# Optimizing a Trainium2 kernel written in Bass

```python
import numpy as np
import jax
import jax.numpy as jnp

def _softmax(x, axis=-1):
    return jax.nn.softmax(x, axis=axis)

def _gelu(x):
    return jax.nn.gelu(x, approximate=True)

def _silu(x):
    return jax.nn.silu(x)

def _sigmoid(x):
    return jax.nn.sigmoid(x)

def _layernorm(x, axis=-1, eps=1e-05):
    m = jnp.mean(x, axis=axis, keepdims=True)
    v = jnp.var(x, axis=axis, keepdims=True)
    return (x - m) / jnp.sqrt(v + eps)

def _scatter_add(tgt, idx, src, axis=0):
    return tgt.at[idx].add(src)

def _segment_sum(src, seg, n):
    return jax.ops.segment_sum(src, seg, n)
kernel_name = 'mk_conv_preact_d2_conv_nchw512_r4_cc65c7'

def setup_inputs(seed: int=0):
    np.random.seed(seed)
    _w = jnp.asarray

    def _rec_inputs():
        import jax
        import jax.numpy as jnp
        _gk = jax.random.key(seed)
        x = -7.109e-05 + 0.9999 * jax.random.normal(jax.random.fold_in(_gk, 1), (32, 128, 16, 16), jnp.float32)
        return x
    x = _rec_inputs()

    def _L0_conv_setup():
        import jax, jax.numpy as jnp
        import numpy as np
        GRID_SIZE = 5
        SPLINE_ORDER = 3
        GRID_RANGE = (-6.0, 6.0)

        def make_grid(in_features):
            h = (GRID_RANGE[1] - GRID_RANGE[0]) / GRID_SIZE
            g = np.arange(-SPLINE_ORDER, GRID_SIZE + SPLINE_ORDER + 1, dtype=np.float32) * h + GRID_RANGE[0]
            return jnp.asarray(np.tile(g[None, :], (in_features, 1)))

        def b_splines(x, grid):
            xg = x[:, :, None]
            bases = ((xg >= grid[:, :-1]) & (xg < grid[:, 1:])).astype(x.dtype)
            for k in range(1, SPLINE_ORDER + 1):
                left = (xg - grid[:, :-(k + 1)]) / (grid[:, k:-1] - grid[:, :-(k + 1)]) * bases[:, :, :-1]
                right = (grid[:, k + 1:] - xg) / (grid[:, k + 1:] - grid[:, 1:-k]) * bases[:, :, 1:]
                bases = left + right
            return bases

        def kan_linear(x, grid, base_w, spline_w, scaler):
            base_out = jax.nn.silu(x) @ base_w.T
            bases = b_splines(x, grid)
            sw = spline_w * scaler[:, :, None]
            spline_out = jnp.einsum('bik,oik->bo', bases, sw)
            return base_out + spline_out
        key = jax.random.key(seed)
        ks = jax.random.split(key, 7)
        b, c, H, W = (32, 128, 16, 16)
        hidden = max(16, c // 8)
        x = jax.random.normal(ks[0], (b, c, H, W), dtype=jnp.float32)
        scale = 0.1
        return {'x': x, 'grid1': make_grid(c), 'base_w1': jax.random.normal(ks[1], (hidden, c), dtype=jnp.float32) * scale, 'spline_w1': jax.random.normal(ks[2], (hidden, c, GRID_SIZE + SPLINE_ORDER), dtype=jnp.float32) * scale, 'scaler1': jax.random.normal(ks[3], (hidden, c), dtype=jnp.float32) * scale + 1.0, 'grid2': make_grid(hidden), 'base_w2': jax.random.normal(ks[4], (c, hidden), dtype=jnp.float32) * scale, 'spline_w2': jax.random.normal(ks[5], (c, hidden, GRID_SIZE + SPLINE_ORDER), dtype=jnp.float32) * scale, 'scaler2': jax.random.normal(ks[6], (c, hidden), dtype=jnp.float32) * scale + 1.0}
    _L0_conv_all = _L0_conv_setup()
    _L0_conv_in = {k: v for k, v in _L0_conv_all.items() if k in ('grid1', 'base_w1', 'spline_w1', 'scaler1', 'grid2', 'base_w2', 'spline_w2', 'scaler2')}
    del _L0_conv_all

    def _L1_conv_setup():
        import jax, jax.numpy as jnp
        import numpy as np
        from jax import lax
        DIM = 128
        MED = 2 * DIM
        NF = 4
        SIZE = 16
        FS = SIZE // 2 + 1
        HR = int(0.5 * DIM)
        HS = int(0.5 * DIM)
        B = 16

        def _conv1x1(x, w, b):
            return jnp.einsum('bchw,oc->bohw', x, w[:, :, 0, 0]) + b[None, :, None, None]

        def _conv3x3(x, w, b):
            return lax.conv_general_dilated(x, w, (1, 1), 'SAME') + b[None, :, None, None]
        key = jax.random.key(seed)
        ks = jax.random.split(key, 12)
        n = lambda k, shape, s=0.02: jax.random.normal(k, shape, jnp.float32) * s
        return dict(x=jax.random.normal(ks[0], (B, DIM, SIZE, SIZE), jnp.float32), w_pw1=n(ks[1], (MED, DIM)), w_pw2=n(ks[2], (DIM, MED)), star_scale=jnp.ones((1,), jnp.float32), star_bias=jnp.zeros((1,), jnp.float32), rw_fc1_w=n(ks[3], (HR, DIM, 1, 1)), rw_fc1_b=jnp.zeros((HR,), jnp.float32), rw_conv_w=n(ks[4], (HR, HR, 1, 1)), rw_conv_b=jnp.zeros((HR,), jnp.float32), rw_fc2_w=n(ks[5], (NF * MED, HR, 1, 1)), rw_fc2_b=jnp.zeros((NF * MED,), jnp.float32), sp_fc1_w=n(ks[6], (HS, DIM, 3, 3)), sp_fc1_b=jnp.zeros((HS,), jnp.float32), sp_fc2_w=n(ks[7], (NF * MED, HS, 3, 3)), sp_fc2_b=jnp.zeros((NF * MED,), jnp.float32), complex_weights=n(ks[8], (SIZE, FS, NF, 2), 0.02), spatial_weights=n(ks[9], (SIZE, SIZE, NF), 0.03))
    _L1_conv_all = _L1_conv_setup()
    _L1_conv_in = {k: v for k, v in _L1_conv_all.items() if k in ('w_pw1', 'w_pw2', 'star_scale', 'star_bias', 'rw_fc1_w', 'rw_fc1_b', 'rw_conv_w', 'rw_conv_b', 'rw_fc2_w', 'rw_fc2_b', 'sp_fc1_w', 'sp_fc1_b', 'sp_fc2_w', 'sp_fc2_b', 'complex_weights', 'spatial_weights')}
    del _L1_conv_all
    return {'x': x, 'L0_conv_grid1': _L0_conv_in['grid1'], 'L0_conv_base_w1': _L0_conv_in['base_w1'], 'L0_conv_spline_w1': _L0_conv_in['spline_w1'], 'L0_conv_scaler1': _L0_conv_in['scaler1'], 'L0_conv_grid2': _L0_conv_in['grid2'], 'L0_conv_base_w2': _L0_conv_in['base_w2'], 'L0_conv_spline_w2': _L0_conv_in['spline_w2'], 'L0_conv_scaler2': _L0_conv_in['scaler2'], 'L1_conv_w_pw1': _L1_conv_in['w_pw1'], 'L1_conv_w_pw2': _L1_conv_in['w_pw2'], 'L1_conv_star_scale': _L1_conv_in['star_scale'], 'L1_conv_star_bias': _L1_conv_in['star_bias'], 'L1_conv_rw_fc1_w': _L1_conv_in['rw_fc1_w'], 'L1_conv_rw_fc1_b': _L1_conv_in['rw_fc1_b'], 'L1_conv_rw_conv_w': _L1_conv_in['rw_conv_w'], 'L1_conv_rw_conv_b': _L1_conv_in['rw_conv_b'], 'L1_conv_rw_fc2_w': _L1_conv_in['rw_fc2_w'], 'L1_conv_rw_fc2_b': _L1_conv_in['rw_fc2_b'], 'L1_conv_sp_fc1_w': _L1_conv_in['sp_fc1_w'], 'L1_conv_sp_fc1_b': _L1_conv_in['sp_fc1_b'], 'L1_conv_sp_fc2_w': _L1_conv_in['sp_fc2_w'], 'L1_conv_sp_fc2_b': _L1_conv_in['sp_fc2_b'], 'L1_conv_complex_weights': _L1_conv_in['complex_weights'], 'L1_conv_spatial_weights': _L1_conv_in['spatial_weights']}

def reference(x, L0_conv_grid1, L0_conv_base_w1, L0_conv_spline_w1, L0_conv_scaler1, L0_conv_grid2, L0_conv_base_w2, L0_conv_spline_w2, L0_conv_scaler2, L1_conv_w_pw1, L1_conv_w_pw2, L1_conv_star_scale, L1_conv_star_bias, L1_conv_rw_fc1_w, L1_conv_rw_fc1_b, L1_conv_rw_conv_w, L1_conv_rw_conv_b, L1_conv_rw_fc2_w, L1_conv_rw_fc2_b, L1_conv_sp_fc1_w, L1_conv_sp_fc1_b, L1_conv_sp_fc2_w, L1_conv_sp_fc2_b, L1_conv_complex_weights, L1_conv_spatial_weights):
    import jax
    import jax.numpy as jnp

    def _L0_conv_ref(x, grid1, base_w1, spline_w1, scaler1, grid2, base_w2, spline_w2, scaler2):
        import jax, jax.numpy as jnp
        import numpy as np
        GRID_SIZE = 5
        SPLINE_ORDER = 3
        GRID_RANGE = (-6.0, 6.0)

        def make_grid(in_features):
            h = (GRID_RANGE[1] - GRID_RANGE[0]) / GRID_SIZE
            g = np.arange(-SPLINE_ORDER, GRID_SIZE + SPLINE_ORDER + 1, dtype=np.float32) * h + GRID_RANGE[0]
            return jnp.asarray(np.tile(g[None, :], (in_features, 1)))

        def b_splines(x, grid):
            xg = x[:, :, None]
            bases = ((xg >= grid[:, :-1]) & (xg < grid[:, 1:])).astype(x.dtype)
            for k in range(1, SPLINE_ORDER + 1):
                left = (xg - grid[:, :-(k + 1)]) / (grid[:, k:-1] - grid[:, :-(k + 1)]) * bases[:, :, :-1]
                right = (grid[:, k + 1:] - xg) / (grid[:, k + 1:] - grid[:, 1:-k]) * bases[:, :, 1:]
                bases = left + right
            return bases

        def kan_linear(x, grid, base_w, spline_w, scaler):
            base_out = jax.nn.silu(x) @ base_w.T
            bases = b_splines(x, grid)
            sw = spline_w * scaler[:, :, None]
            spline_out = jnp.einsum('bik,oik->bo', bases, sw)
            return base_out + spline_out
        b, c = (x.shape[0], x.shape[1])
        s = jnp.mean(x, axis=(2, 3))
        s = jnp.nan_to_num(s)
        s = kan_linear(s, grid1, base_w1, spline_w1, scaler1)
        s = jax.nn.silu(s)
        s = kan_linear(s, grid2, base_w2, spline_w2, scaler2)
        gate = jax.nn.sigmoid(s).reshape(b, c, 1, 1)
        return x * gate

    def _L1_conv_ref(x, w_pw1, w_pw2, star_scale, star_bias, rw_fc1_w, rw_fc1_b, rw_conv_w, rw_conv_b, rw_fc2_w, rw_fc2_b, sp_fc1_w, sp_fc1_b, sp_fc2_w, sp_fc2_b, complex_weights, spatial_weights):
        import jax, jax.numpy as jnp
        import numpy as np
        from jax import lax
        DIM = 128
        MED = 2 * DIM
        NF = 4
        SIZE = 16
        FS = SIZE // 2 + 1
        HR = int(0.5 * DIM)
        HS = int(0.5 * DIM)
        B = 16

        def _conv1x1(x, w, b):
            return jnp.einsum('bchw,oc->bohw', x, w[:, :, 0, 0]) + b[None, :, None, None]

        def _conv3x3(x, w, b):
            return lax.conv_general_dilated(x, w, (1, 1), 'SAME') + b[None, :, None, None]
        Bn, _, H, W = x.shape
        r = jax.nn.relu(_conv1x1(x, rw_fc1_w, rw_fc1_b))
        r = jax.nn.relu(_conv1x1(r, rw_conv_w, rw_conv_b))
        r = _conv1x1(r, rw_fc2_w, rw_fc2_b)
        routeing = jax.nn.softmax(r.mean(axis=(2, 3)).reshape(Bn, NF, MED), axis=1)
        s = jax.nn.relu(_conv3x3(x, sp_fc1_w, sp_fc1_b))
        s = _conv3x3(s, sp_fc2_w, sp_fc2_b)
        spatial_routeing = jax.nn.softmax(s.mean(axis=(2, 3)).reshape(Bn, NF, MED), axis=1)
        xc = jnp.transpose(x, (0, 2, 3, 1))
        xp = jnp.einsum('bhwc,mc->bhwm', xc, w_pw1)
        xp = star_scale * jnp.square(jax.nn.relu(xp)) + star_bias
        xf = jnp.fft.rfft2(xp, axes=(1, 2), norm='ortho')
        cw = lax.complex(complex_weights[..., 0], complex_weights[..., 1])
        weight = jnp.einsum('bfc,hwf->bhwc', routeing.astype(cw.dtype), cw)
        spatial_weight = jnp.einsum('bfc,hwf->bhwc', spatial_routeing, spatial_weights)
        xs = jnp.fft.irfft2(xf * weight, s=(H, W), axes=(1, 2), norm='ortho')
        out = xp * spatial_weight + xs
        out = jnp.einsum('bhwm,dm->bhwd', out, w_pw2)
        return jnp.transpose(out, (0, 3, 1, 2))

    def _gn(v, G=32, eps=1e-05):
        B_, C_, H_, W_ = v.shape
        g = v.reshape(B_, G, C_ // G, H_, W_)
        m = jnp.mean(g, axis=(2, 3, 4), keepdims=True)
        s = jnp.var(g, axis=(2, 3, 4), keepdims=True)
        return ((g - m) / jnp.sqrt(s + eps)).reshape(v.shape)

    def _ln_c(v, eps=1e-06):
        m = jnp.mean(v, axis=1, keepdims=True)
        s = jnp.var(v, axis=1, keepdims=True)
        return (v - m) / jnp.sqrt(s + eps)

    def _ln_t(v, eps=1e-05):
        m = jnp.mean(v, axis=-1, keepdims=True)
        s = jnp.var(v, axis=-1, keepdims=True)
        return (v - m) / jnp.sqrt(s + eps)

    def _to_tokens(v):
        B_, C_, H_, W_ = v.shape
        return v.reshape(B_, C_, H_ * W_).transpose(0, 2, 1)

    def _from_tokens(t, like):
        B_, C_, H_, W_ = like.shape
        return t.transpose(0, 2, 1).reshape(B_, C_, H_, W_)
    x = x + _L0_conv_ref(_gn(x), L0_conv_grid1, L0_conv_base_w1, L0_conv_spline_w1, L0_conv_scaler1, L0_conv_grid2, L0_conv_base_w2, L0_conv_spline_w2, L0_conv_scaler2)
    x = x + _L1_conv_ref(_gn(x), L1_conv_w_pw1, L1_conv_w_pw2, L1_conv_star_scale, L1_conv_star_bias, L1_conv_rw_fc1_w, L1_conv_rw_fc1_b, L1_conv_rw_conv_w, L1_conv_rw_conv_b, L1_conv_rw_fc2_w, L1_conv_rw_fc2_b, L1_conv_sp_fc1_w, L1_conv_sp_fc1_b, L1_conv_sp_fc2_w, L1_conv_sp_fc2_b, L1_conv_complex_weights, L1_conv_spatial_weights)
    return x

_drawn_inputs = setup_inputs


def setup_inputs(seed=0):
    import zlib

    import numpy as np

    out = dict(_drawn_inputs(seed))
    spreads = {'L1_conv_rw_fc1_b': (0.0, 0.8),
     'L1_conv_rw_conv_b': (0.0, 0.8),
     'L1_conv_rw_fc2_b': (0.0, 0.8),
     'L1_conv_sp_fc1_b': (0.0, 0.8),
     'L1_conv_sp_fc2_b': (0.0, 0.8)}
    factors = {'L0_conv_grid1': 6.513,
     'L0_conv_base_w1': 47.687,
     'L0_conv_spline_w1': 4.834,
     'L0_conv_scaler1': 8.0,
     'L0_conv_base_w2': 3.074,
     'L0_conv_scaler2': 58.989,
     'L1_conv_w_pw1': 8.0,
     'L1_conv_w_pw2': 8.0,
     'L1_conv_rw_fc1_w': 21.804,
     'L1_conv_rw_conv_w': 8.0,
     'L1_conv_rw_fc2_w': 8.0,
     'L1_conv_sp_fc1_w': 8.0,
     'L1_conv_sp_fc2_w': 8.0,
     'L1_conv_complex_weights': 8.0,
     'L1_conv_spatial_weights': 8.0}
    for name, (base, spread) in spreads.items():
        noise = np.random.default_rng([zlib.crc32(name.encode()), seed]).standard_normal(out[name].shape)
        drawn = base * np.exp(spread * noise) if base else spread * noise
        out[name] = jnp.asarray(drawn.astype(out[name].dtype))
    for name, factor in factors.items():
        out[name] = (out[name] * factor).astype(out[name].dtype)
    return out
```

```python
from contextlib import ExitStack

import numpy as np

import concourse.bass as bass
from concourse import mybir

F32 = mybir.dt.float32
F16 = mybir.dt.float16
BF16 = mybir.dt.bfloat16
I32 = mybir.dt.int32
ALU = mybir.AluOpType
ACT = mybir.ActivationFunctionType
AX = mybir.AxisListType.X

P = 128
NB = 32
C = 128
SIDE = 16
HW = SIDE * SIDE
MED = 2 * C
NF = 4
HID = 64
TAPS = 9
PAD = SIDE + 2
KH = 16
KNOTS = 12
ORDER = 3
NK = KNOTS - 1 - ORDER
GROUP = 4
EPS = 1e-5
FMAX = 3.4028235e38

IT = 4
NIT = NB // IT
PAIRS = 5
GROUPS = 6
LEFT_PART = [0, 0, 0, 1, 1, 2]
RIGHT_PART = [0, 1, 2, 0, 1, 0]
X_CHUNKS = 8


def pair_tap(p):
    return min(2 * p, TAPS - 2)


def slots():
    inner = range(1, SIDE // 2)
    half = SIDE // 2
    found = [((0, 0), (0, half)), ((half, 0), (half, half))]
    for first in (0, 1):
        for ky in range(first, SIDE, 2):
            found += [((ky, kx), (ky, kx)) for kx in inner]
        for ky in range(first, half, 2):
            if ky:
                found += [((ky, kx), (ky, kx)) for kx in (0, half)]
    assert len(found) == P
    return found


def constants():
    half = SIDE // 2
    fs = half + 1
    ident = np.eye(P)
    group = np.kron(np.eye(P // GROUP), np.full((GROUP, GROUP), 1.0 / GROUP))
    h, w = np.divmod(np.arange(HW), SIDE)
    forward = np.zeros((P, 2, 2, 64))
    inverse = np.zeros((P, 2, HW))
    sym = np.zeros((SIDE, fs, 2, 2, P))
    for n, (fa, fb) in enumerate(slots()):
        odd, col = divmod(n, 64)
        real = fa != fb
        for part, (ky, kx) in enumerate((fa, fb)):
            angle = 2 * np.pi * (ky * h + kx * w) / SIDE
            wave = np.cos(angle) if real or part == 0 else -np.sin(angle)
            forward[:, odd, part, col] = wave[:P] / SIDE
            inverse[n, part] = wave * (1 if real else 2) / SIDE
            re_im = 0 if real else part
            if real or kx not in (0, half):
                sym[ky, kx, re_im, part, n] = 1
            else:
                sym[ky, kx, re_im, part, n] = 0.5
                sym[(SIDE - ky) % SIDE, kx, re_im, part, n] = 0.5 if re_im == 0 else -0.5
    sym = sym.reshape(2, SIDE * fs // 2, 2, 2 * P).transpose(1, 0, 2, 3).reshape(SIDE * fs // 2, -1)
    return {
        "ident": ident, "group": group, "forward": forward.reshape(P, -1),
        "inverse": inverse.reshape(P, -1), "sym": sym,
    }


class Steps:

    def __init__(self, eng, sem):
        self.eng, self.sem, self.base, self.n = eng, sem, 0, 0

    def did(self, ins):
        ins.then_inc(self.sem, 1)
        self.n += 1

    def settle(self):
        self.eng.wait_ge(self.sem, self.base + self.n)

    def then(self, ins):
        self.did(ins)
        self.settle()

    def enter(self, start, i, per):
        self.base, self.n = start + i * per, 0

    def leave(self, start, rounds, per):
        assert self.n == per, self.n
        self.base, self.n = start + rounds * per, 0


def build(nc, x, grid1, base_w1, spline_w1, scaler1, grid2, base_w2, spline_w2, scaler2, w_pw1, w_pw2,
          star_scale, star_bias, rw_fc1_w, rw_fc1_b, rw_conv_w, rw_conv_b, rw_fc2_w, rw_fc2_b,
          sp_fc1_w, sp_fc1_b, sp_fc2_w, sp_fc2_b, complex_w, spatial_w,
          c_ident, c_group, c_forward, c_inverse, c_sym, out):
    ctx = ExitStack()
    with ctx:
        def sb(name, shape, dt=F32):
            return ctx.enter_context(nc.sbuf_tensor(name, shape, dt))

        def ps(name, shape, dt=F32):
            return ctx.enter_context(nc.psum_tensor(name, shape, dt))

        def sem(name):
            return ctx.enter_context(nc.semaphore(name))

        x_all = sb("x_all", [P, NB, HW])
        z_all = sb("z_all", [P, NB, 2, HW], F16)
        ident = sb("ident_sb", [P, P])
        ident_b = sb("ident_b", [P, P], BF16)
        group = sb("group_sb", [P, P])
        forward = sb("forward_sb", [P, 2, 2, 64])
        inverse = sb("inverse_sb", [P, 2, HW])
        coef = sb("coef", [P, 4, NB])
        bcast = sb("bcast", [P, 3])
        eps = sb("eps", [P, 1])
        ones = sb("ones", [1, P])
        pw1_f = sb("pw1_f", [P, MED])
        pw1_h = sb("pw1_h", [P, MED], F16)
        pw1_l = sb("pw1_l", [P, MED], F16)
        misc_t = sb("misc_t", [P, 400])
        pw2_t = misc_t[:, 0:256].rearrange("m (t d) -> m t d", t=2)
        rwc_t = misc_t[:, 256:384]
        bias_t = misc_t[:, 384:400]
        filters = sb("filters", [P, 512], BF16)
        kan1_nat = sb("kan1_nat", [KH, NK + 1, C])
        kan1_sp = sb("kan1_sp", [KH, C, NK])
        kan1_sc = sb("kan1_sc", [KH, C])
        grid1_sb = sb("grid1_sb", [C, KNOTS])
        kan2_nat = sb("kan2_nat", [C, NK + 1, KH])
        kan2_sp = sb("kan2_sp", [C, KH, NK])
        kan2_sc = sb("kan2_sc", [C, KH])
        grid2_sb = sb("grid2_sb", [KH, KNOTS])
        sp_perm = sb("sp_perm", [P, 8, TAPS, HID])
        shared = sp_perm[:, :, :, :].rearrange("p t k i -> p (t k i)")
        taken = [0]

        def part_of_shared(*shape):
            size = int(np.prod(shape))
            lo = taken[0]
            taken[0] += size
            assert taken[0] <= 8 * TAPS * HID
            flat = shared[:, lo:lo + size]
            if len(shape) == 1:
                return flat
            if len(shape) == 2:
                return flat.rearrange("p (a b) -> p a b", a=shape[0])
            return flat.rearrange("p (a b c) -> p a b c", a=shape[0], b=shape[1])

        conv_nat = part_of_shared(C * TAPS)
        rw1_nat = sb("rw1_nat", [P, C])
        rwc_nat = sb("rwc_nat", [P, P])
        pw1_nat = sb("pw1_nat", [P, 2, C])
        pw2_nat = sb("pw2_nat", [C, MED])
        rwf_nat = sb("rwf_nat", [P, 8, HID])
        bias_nat = sb("bias_nat", [16, P])
        bias_col = sb("bias_col", [P, 3])
        star = sb("star", [1, 3])
        cw_sb = sb("cw_sb", [72, 2, NF * 2])
        sw_nat = sb("sw_nat", [P, 2, NF])
        sym_sb = part_of_shared(2, 2, 2 * P)[0:72]
        sp_nat = sb("sp_nat", [P, 8, HID * TAPS])
        kan1_t = sb("kan1_t", [C, NK + 1, KH])
        kan2_t = sb("kan2_t", [KH, NK + 1, C])
        conv_f = sb("conv_f", [P, TAPS + 1, HID])
        conv_h = sb("conv_h", [P, TAPS + 1, HID], F16)
        conv_l = sb("conv_l", [P, TAPS + 1, HID], F16)
        amax = sb("amax", [P, 2])
        rmax = sb("rmax", [P, 3])
        rwf_t = sb("rwf_t", [HID, 8, P])
        sp_t = sb("sp_t", [P, 8, PAIRS, P])
        stats = sb("stats", [P, NB, 6])
        mean = sb("mean", [P, NB])
        var = sb("var", [P, NB])
        g_mean = sb("g_mean", [P, NB])
        small = sb("small", [P, 8, NB])
        nan_mask = sb("nan_mask", [P, NB], I32)
        k_inv = sb("k_inv", [P, 2, ORDER, KNOTS - 1])
        k_den = sb("k_den", [P, 2, ORDER, KNOTS - 1])
        k_dist = part_of_shared(KNOTS, NB)
        k_ge = part_of_shared(KNOTS, NB)
        k_lt = part_of_shared(KNOTS, NB)
        k_bas = part_of_shared(KNOTS - 1, NB)
        k_m = part_of_shared(KNOTS - 1, NB)
        k_rhs = part_of_shared(NK + 1, NB)
        k_in = sb("k_in", [P, 3, NB])
        zpads = sb("zpads", [P, 2, 2, IT, PAD, PAD], F16)
        zpad = [zpads[:, u] for u in range(2)]
        z32 = sb("z32", [P, IT, HW])
        r1 = sb("r1", [P, 512])
        s1 = sb("s1", [P, 2, SIDE, SIDE])
        r2 = sb("r2", [P, 2, HW], BF16)
        r2_pair = sb("r2_pair", [P, 2])
        r2_sum = sb("r2_sum", [P, NIT, 2])
        rows = sb("rows", [P, 3, 2, SIDE])
        win = sb("win", [P, 3, 3, NIT, 2])
        win_p = sb("win_p", [P, PAIRS, NB])
        r2_p = sb("r2_p", [HID, NB])
        rt_max = sb("rt_max", [P, 4, 2 * NB])
        rt_part = [sb(f"rt_part{n}", [P, 2 * 8, NB], BF16) for n in range(2)]
        route = sb("route", [P, NB, 2, P], BF16)
        f_cols = sb("f_cols", [P, 4, P], BF16)
        f_res = sb("f_res", [P, 4, NF])
        f_part = sb("f_part", [P, 3, 4, NF], BF16)
        z_space = zpads[:, :, :, :, :, :].rearrange("p u l k h w -> p (u l k h w)")
        logit = z_space[:, 0:1024].bitcast(F32).rearrange("p (t b) -> p t b", b=NB)
        rt_res = z_space[:, 1024:2048].bitcast(F32).rearrange("p (t b) -> p t b", b=NB)
        rt_cols = z_space[:, 2048:2048 + NB * 2 * 8 * GROUPS].bitcast(BF16).rearrange("p (b m c) -> p b m c", b=NB, m=2)
        sp_space = sp_nat[:, :, :].rearrange("p t c -> p (t c)")
        relu_v, sq_v, xp, eo, spec, t_re, prod, swt, qt = (sp_space[:, 512 * n:512 * n + 512] for n in range(9))
        xp, eo, swt, qt = (a.rearrange("p (t m) -> p t m", t=2) for a in (xp, eo, swt, qt))
        spec, t_re, prod = (a.rearrange("p (m a s) -> p m a s", m=2, a=2) for a in (spec, t_re, prod))
        t_im = sb("t_im", [P, 2, 2, P])
        y_sb = sb("y_sb", [P, 2, C])

        bank = [ps(f"bank{n}", [P, 512])[:, :] for n in range(8)]
        mixed_slot = bank[3].rearrange("p (m a s) -> p m a s", m=2, a=2)
        mixed_pixel = bank[4].rearrange("p (m s) -> p m s", m=2)

        in_x = [sem(f"in_x{n}") for n in range(X_CHUNKS)]
        in_kan, in_conv, in_misc, in_const, in_sp, in_rwc, sp_ready = (sem(n) for n in (
            "in_kan", "in_conv", "in_misc", "in_const", "in_sp", "in_rwc", "sp_ready"))
        zeroed, const_set = sem("zeroed"), sem("const_set")
        dve_step, act_step, pool_step = sem("dve_step"), sem("act_step"), sem("pool_step")
        kan_nat_ready, conv_nat_ready = sem("kan_nat_ready"), sem("conv_nat_ready")
        prep_done, prep_out = sem("prep_done"), sem("prep_out")
        conv_parts, pw1_parts = sem("conv_parts"), sem("pw1_parts")
        max_col, max_row, star_ready, bcast_done = (sem(n) for n in ("max_col", "max_row", "star_ready", "bcast_done"))
        filt_done, filt_cols, filt_ready = sem("filt_done"), sem("filt_cols"), sem("filt_ready")
        gm_in, gm_out = sem("gm_in"), sem("gm_out")
        var_ready, std_ready = sem("var_ready"), sem("std_ready")
        kan_in, kan_sig, kan_rhs, kan_done = sem("kan_in"), sem("kan_sig"), sem("kan_rhs"), sem("kan_done")
        coef_ready = sem("coef_ready")
        zh_ready, zl_ready, z_kept = sem("zh_ready"), sem("zl_ready"), sem("z_kept")
        rw1_done, conv_done, rwc_done = sem("rw1_done"), sem("conv_done"), sem("rwc_done")
        r1_ready, s1_ready, r2_ready = sem("r1_ready"), sem("s1_ready"), sem("r2_ready")
        r2_kept, win_ready = sem("r2_kept"), sem("win_ready")
        sums_ready, logits_done, soft_in, soft_exp = (sem(n) for n in ("sums_ready", "logits_done", "soft_in", "soft_exp"))
        rt_ready, rt_dup, rt_done = sem("rt_ready"), sem("rt_dup"), sem("rt_done")
        rt_out = [sem("rt_out_act"), sem("rt_out_dve")]
        v_done, relu_ready, sq_ready, xp_ready, eo_ready = (sem(n) for n in (
            "v_done", "relu_ready", "sq_ready", "xp_ready", "eo_ready"))
        dft_done, xt_done, w_done, spec_ready, sw_ready = (sem(n) for n in (
            "dft_done", "xt_done", "w_done", "spec_ready", "sw_ready"))
        terms_ready, prod_ready, qt_ready, y_done, y_ready = (sem(n) for n in (
            "terms_ready", "prod_ready", "qt_ready", "y_done", "y_ready"))
        sp_done, out_done, fin_ready, stored = (sem(n) for n in ("sp_done", "out_done", "fin_ready", "stored"))

        KAN_LOADS, CONV_LOADS, MISC_LOADS, CONST_LOADS = 8, 4, 15, 5
        PREP_ACT = 10
        SP_GROUPS = 10

        def one(ap, n):
            if isinstance(n, int):
                return ap[:, n]
            return ap[:, bass.ds(n, 1)].squeeze(1)

        block = ctx.enter_context(nc.Block())

        @block.sync
        def _(sp):
            for n in range(X_CHUNKS):
                k = NB // X_CHUNKS
                sp.dma_start(x_all[:, n * k:(n + 1) * k, :],
                             x[n * k:(n + 1) * k].rearrange("b c h w -> c b (h w)")).then_inc(in_x[n], 16)
            sp_rows = sp_fc2_w.rearrange("(t p) i a b -> p t (i a b)", p=P)
            for n in range(2):
                sp.dma_start(sp_nat[:, 4 * n:4 * n + 4, :], sp_rows[:, 4 * n:4 * n + 4, :]).then_inc(in_sp, 16)
            out_v = out.rearrange("b c h w -> c b (h w)")
            with sp.Fori(0, NB) as i:
                sp.wait_ge(fin_ready, i + 1)
                sp.dma_start(one(out_v, i), one(x_all, i)).then_inc(stored, 16)
            sp.wait_ge(stored, 16 * NB)

        @block.gpsimd
        def _(pool):
            steps = Steps(pool, pool_step)
            pool.memset(rwc_nat[:, :], 0.0).then_inc(zeroed, 1)
            pool.memset(f_cols[:, :, :], 0.0).then_inc(zeroed, 1)
            pool.memset(zpads[:, :, :, :, :, :], 0.0).then_inc(zeroed, 1)
            pool.memset(route[:, :, :, :], 0.0).then_inc(zeroed, 1)
            pool.memset(win_p[:, PAIRS - 1, :], 0.0).then_inc(zeroed, 1)
            pool.memset(t_im[:, :, :, :], 0.0).then_inc(zeroed, 1)
            pool.wait_ge(prep_out, 2)
            steps.then(pool.tensor_copy(conv_h[:, :, :], conv_f[:, :, :]))
            pool.tensor_tensor(conv_l[:, :, :], conv_f[:, :, :], conv_h[:, :, :], ALU.subtract).then_inc(conv_parts, 1)

            def products(i):
                pool.wait_ge(terms_ready, 3 * i + 3)
                if not isinstance(i, int) or i >= 1:
                    pool.wait_ge(y_done, i)
                pool.tensor_tensor(prod[:, :, 0, :], t_re[:, :, 0, :], t_im[:, :, 1, :], ALU.subtract).then_inc(prod_ready, 1)
                pool.tensor_tensor(prod[:, :, 1, :], t_re[:, :, 1, :], t_im[:, :, 0, :], ALU.add).then_inc(prod_ready, 1)

            pool.wait_ge(in_sp, 32)
            pool.wait_ge(coef_ready, 1)
            for t in range(8):
                pool.tensor_copy(sp_perm[:, t, :, :], sp_nat[:, t, :].rearrange("o (i k) -> o k i", k=TAPS)).then_inc(sp_ready, 1)

            products(0)
            with pool.Fori(1, NB - 1) as i:
                products(i)
            products(NB - 1)

        @block.scalar
        def _(act):
            steps = Steps(act, act_step)
            act.dma_start(ident[:, :], c_ident).then_inc(in_const, 16)
            for dst, src in ((kan1_sp[:, :, :], spline_w1), (kan1_sc[:, :], scaler1), (kan1_nat[:, NK, :], base_w1),
                             (grid1_sb[:, :], grid1), (kan2_sp[:, :, :], spline_w2), (kan2_sc[:, :], scaler2),
                             (kan2_nat[:, NK, :], base_w2), (grid2_sb[:, :], grid2)):
                act.dma_start(dst, src).then_inc(in_kan, 16)
            for half in range(2):
                rows_of = slice(HID * half, HID * half + HID)
                act.dma_start(conv_nat[rows_of, :], sp_fc1_w.rearrange("o i a b -> o (i a b)")).then_inc(in_conv, 16)
                act.dma_start(rw1_nat[rows_of, :], rw_fc1_w.rearrange("o i a b -> o (i a b)")).then_inc(in_conv, 16)
            act.dma_start(group[:, :], c_group).then_inc(in_const, 16)
            act.dma_start(forward[:, :, :, :], c_forward.rearrange("p (a b c) -> p a b c", a=2, b=2)).then_inc(in_const, 16)
            act.dma_start(inverse[:, :, :], c_inverse.rearrange("p (a b) -> p a b", a=2)).then_inc(in_const, 16)
            act.dma_start(sym_sb[:, :, :, :], c_sym.rearrange("p (a b c) -> p a b c", a=2, b=2)).then_inc(in_const, 16)
            act.dma_start(pw1_nat[:, :, :], w_pw1.rearrange("(t p) c -> p t c", p=P)).then_inc(in_misc, 16)
            act.dma_start(pw2_nat[:, :], w_pw2).then_inc(in_misc, 16)
            act.dma_start(rwf_nat[:, :, :], rw_fc2_w.rearrange("(t p) i a b -> p t (i a b)", p=P)).then_inc(in_misc, 16)
            act.dma_start(bias_nat[0:8, :], sp_fc2_b.rearrange("(t p) -> t p", p=P)).then_inc(in_misc, 16)
            act.dma_start(bias_nat[8:16, :], rw_fc2_b.rearrange("(t p) -> t p", p=P)).then_inc(in_misc, 16)
            for half in range(2):
                rows_of = slice(HID * half, HID * half + HID)
                for n, src in enumerate((sp_fc1_b, rw_fc1_b, rw_conv_b)):
                    act.dma_start(bias_col[rows_of, n:n + 1], src.rearrange("(p a) -> p a", a=1)).then_inc(in_misc, 16)
            act.dma_start(star[:, 0:1], star_scale.rearrange("(p a) -> p a", a=1)).then_inc(in_misc, 16)
            act.dma_start(star[:, 1:2], star_bias.rearrange("(p a) -> p a", a=1)).then_inc(in_misc, 16)
            act.dma_start(cw_sb[:, :, :], complex_w.rearrange("(u k) x f c -> (k x) u (f c)", u=2)).then_inc(in_misc, 16)
            act.dma_start(sw_nat[:, :, :], spatial_w.rearrange("(u k) w f -> (k w) u f", u=2)).then_inc(in_misc, 16)
            act.wait_ge(zeroed, 1)
            for half in range(2):
                rows_of = slice(HID * half, HID * half + HID)
                act.dma_start(rwc_nat[rows_of, rows_of], rw_conv_w.rearrange("o i a b -> o (i a b)")).then_inc(in_rwc, 16)

            outs = [(conv_f[:, 0:8, :].rearrange("p t o -> p (t o)"), P, 512),
                    (conv_f[:, 8:10, :].rearrange("p t o -> p (t o)"), P, 128),
                    (kan1_t[:, :, :].rearrange("p k o -> p (k o)"), C, (NK + 1) * KH),
                    (kan2_t[:, 0:4, :].rearrange("p k o -> p (k o)"), KH, 512),
                    (kan2_t[:, 4:8, :].rearrange("p k o -> p (k o)"), KH, 512),
                    (kan2_t[:, 8, :], KH, 128),
                    (pw1_f[:, :], P, MED),
                    (misc_t[:, :], P, 400),
                    (rwf_t[:, 0:4, :].rearrange("p t o -> p (t o)"), HID, 512),
                    (rwf_t[:, 4:8, :].rearrange("p t o -> p (t o)"), HID, 512)]
            assert len(outs) == PREP_ACT
            for n, (dst, rows_n, cols) in enumerate(outs):
                act.wait_ge(prep_done, n + 1)
                act.activation(dst, bank[n % 4][0:rows_n, 0:cols], ACT.Identity).then_inc(prep_out, 1)
            act.wait_ge(filt_done, 2)
            act.activation(filters[:, :], bank[4].bitcast(BF16)[:, 0:512], ACT.Identity).then_inc(filt_ready, 1)

            act.wait_ge(const_set, 1)
            act.wait_ge(var_ready, 1)
            act.activation(small[:, 0, :], bank[6][:, 0:NB], ACT.Sqrt, bias=eps[:, 0:1]).then_inc(std_ready, 1)
            act.wait_ge(kan_in, 1)
            act.activation(k_in[:, 1, :], k_in[:, 0, :], ACT.Sigmoid).then_inc(kan_sig, 1)
            act.wait_ge(kan_done, 1)
            act.activation(k_in[0:KH, 1, :], bank[7][0:KH, 0:NB], ACT.Sigmoid).then_inc(kan_sig, 1)
            act.wait_ge(kan_in, 2)
            act.activation(k_in[0:KH, 1, :], k_in[0:KH, 0, :], ACT.Sigmoid).then_inc(kan_sig, 1)
            act.wait_ge(kan_done, 2)
            act.activation(k_in[:, 1, :], bank[7][:, 64:64 + NB], ACT.Sigmoid).then_inc(kan_sig, 1)
            act.wait_ge(var_ready, 2)
            act.activation(small[:, 0, :], bank[6][:, 0:NB], ACT.Sqrt, bias=eps[:, 0:1]).then_inc(std_ready, 1)

            def z_high(it, u):
                if not isinstance(it, int) or it >= 2:
                    act.wait_ge(conv_done, it - 1)
                    act.wait_ge(rw1_done, it - 1)
                    act.wait_ge(z_kept, 2 * it - 2)
                for k in range(IT):
                    b = it * IT + k
                    act.activation(zpad[u][:, 0, k, 1:SIDE + 1, 1:SIDE + 1],
                                   one(x_all, b).rearrange("p (h w) -> p h w", w=SIDE), ACT.Identity,
                                   bias=one(coef[:, 3, :].unsqueeze(2), b),
                                   scale=one(coef[:, 2, :].unsqueeze(2), b)).then_inc(zh_ready, 1)

            def hidden(it, u):
                act.wait_ge(rw1_done, it + 1)
                if not isinstance(it, int) or it >= 1:
                    act.wait_ge(rwc_done, it)
                act.activation(r1[:, :], bank[2 + u], ACT.Relu, bias=bias_col[:, 1:2], scale=amax[:, 1:2]).then_inc(r1_ready, 1)
                act.wait_ge(conv_done, it + 1)
                if not isinstance(it, int) or it >= 1:
                    act.wait_ge(win_ready, it)
                    act.wait_ge(r2_kept, it)
                act.activation(s1[:, :, :, :].rearrange("p j h w -> p (j h w)"), bank[u], ACT.Relu,
                               bias=bias_col[:, 0:1], scale=amax[:, 0:1]).then_inc(s1_ready, 1)
                act.wait_ge(rwc_done, it + 1)
                if not isinstance(it, int) or it >= 1:
                    act.wait_ge(r2_ready, 2 * it)
                for j in range(2):
                    act.activation(r2[:, j, :], bank[5 + u][:, j * HW:(j + 1) * HW], ACT.Relu,
                                   bias=bias_col[:, 2:3], accum_out=r2_pair[:, j:j + 1]).then_inc(r2_ready, 1)

            act.wait_ge(zeroed, 3)
            act.wait_ge(coef_ready, 1)
            act.wait_ge(in_misc, 16 * MISC_LOADS)
            z_high(0, 0)
            z_high(1, 1)
            hidden(0, 0)
            with act.Fori(1, NIT // 2) as j:
                z_high(2 * j, 0)
                hidden(2 * j - 1, 1)
                z_high(2 * j + 1, 1)
                hidden(2 * j, 0)
            hidden(NIT - 1, 1)

            def relu_square(i):
                act.wait_ge(v_done, i + 1)
                if not isinstance(i, int) or i >= 1:
                    act.wait_ge(sq_ready, i)
                act.activation(relu_v[:, :], bank[0], ACT.Relu, scale=bcast[:, 2:3]).then_inc(relu_ready, 1)
                act.wait_ge(relu_ready, i + 1)
                if not isinstance(i, int) or i >= 1:
                    act.wait_ge(xp_ready, i)
                act.activation(sq_v[:, :], relu_v[:, :], ACT.Square).then_inc(sq_ready, 1)

            def spectrum(i):
                act.wait_ge(dft_done, i + 1)
                if not isinstance(i, int) or i >= 1:
                    act.wait_ge(terms_ready, 3 * i)
                act.activation(spec[:, :, :, :].rearrange("p m a s -> p (m a s)"), bank[1], ACT.Identity).then_inc(spec_ready, 1)

            def spatial_mix(i):
                act.wait_ge(w_done, i + 1)
                if not isinstance(i, int) or i >= 1:
                    act.wait_ge(qt_ready, i)
                act.activation(swt[:, :, :], mixed_pixel, ACT.Identity).then_inc(sw_ready, 1)

            def y_copy(i):
                act.wait_ge(y_done, i + 1)
                if not isinstance(i, int) or i >= 1:
                    act.wait_ge(out_done, i)
                act.activation(y_sb[:, :, :].rearrange("p a d -> p (a d)"), bank[5][:, 0:2 * C], ACT.Identity).then_inc(y_ready, 1)

            for n in range(SP_GROUPS):
                act.wait_ge(prep_done, PREP_ACT + n + 1)
                act.activation(sp_t[:, :, :, :].rearrange("p t q o -> p (t q o)")[:, 512 * n:512 * n + 512],
                               bank[5 + n % 2], ACT.Identity).then_inc(prep_out, 1)
            relu_square(0)
            spectrum(0)
            act.wait_ge(soft_in, 1)
            act.activation(logit, logit, ACT.Exp).then_inc(soft_exp, 1)
            relu_square(1)
            copies = 0
            for g in range(GROUPS):
                part = LEFT_PART[g]
                if g in (0, 3, 5):
                    continue
                act.wait_ge(rt_ready, part + 1)
                act.activation(rt_cols[:, :, :, g * 8:g * 8 + 8].rearrange("p b m c -> p c m b"),
                               rt_part[part][:, :, :].rearrange("p (c m) b -> p c m b", m=2), ACT.Identity).then_inc(rt_dup, 1)
                copies += 1
            assert copies == 3
            for n in range(0, NIT, 2):
                act.wait_ge(rt_done, n + 1)
                act.activation(route[0:8 * GROUPS, n * IT:(n + 1) * IT, :, :].rearrange("p b m c -> p (b m c)"),
                               bank[5][0:8 * GROUPS].bitcast(BF16), ACT.Identity).then_inc(rt_out[0], 1)
            spatial_mix(0)

            def round_of(i):
                relu_square(i + 2)
                spectrum(i + 1)
                spatial_mix(i + 1)
                y_copy(i)

            round_of(0)
            with act.Fori(1, NB - 2) as i:
                round_of(i)
            spectrum(NB - 1)
            spatial_mix(NB - 1)
            y_copy(NB - 2)
            y_copy(NB - 1)

        @block.vector
        def _(dve):
            steps = Steps(dve, dve_step)
            tt = dve.tensor_tensor

            dve.memset(eps[:, :], EPS).then_inc(const_set, 1)
            dve.memset(ones[:, :], 1.0).then_inc(const_set, 1)
            dve.wait_ge(in_kan, 16 * KAN_LOADS)
            tt(kan1_nat[:, 0:NK, :].rearrange("o k i -> o i k"), kan1_sp[:, :, :],
               kan1_sc[:, :].unsqueeze(2).broadcast_to([KH, C, NK]), ALU.mult).then_inc(kan_nat_ready, 1)
            tt(kan2_nat[:, 0:NK, :].rearrange("o k i -> o i k"), kan2_sp[:, :, :],
               kan2_sc[:, :].unsqueeze(2).broadcast_to([C, KH, NK]), ALU.mult).then_inc(kan_nat_ready, 1)
            for layer, (n, grid) in enumerate(((C, grid1_sb), (KH, grid2_sb))):
                for k in range(1, ORDER + 1):
                    steps.did(tt(k_den[0:n, layer, k - 1, 0:KNOTS - k], grid[:, k:KNOTS], grid[:, 0:KNOTS - k], ALU.subtract))
            steps.settle()
            for layer, n in ((0, C), (1, KH)):
                for k in range(1, ORDER + 1):
                    steps.did(dve.reciprocal(k_inv[0:n, layer, k - 1, 0:KNOTS - k], k_den[0:n, layer, k - 1, 0:KNOTS - k]))
            dve.wait_ge(in_conv, 16 * CONV_LOADS)
            for n, w in enumerate((conv_nat, rw1_nat)):
                steps.did(dve.tensor_reduce(amax[:, n:n + 1], w[:, :], AX, ALU.max, apply_absolute_value=True))
            steps.settle()
            steps.then(dve.tensor_scalar(amax[:, :], amax[:, :], 1e-30, None, ALU.max))
            steps.then(dve.reciprocal(rmax[:, 0:2], amax[:, :]))
            for n, w in enumerate((conv_nat, rw1_nat)):
                dve.tensor_scalar(w[:, :], w[:, :], rmax[:, n:n + 1], None, ALU.mult).then_inc(conv_nat_ready, 1)
            dve.wait_ge(in_const, 16 * CONST_LOADS)
            dve.tensor_copy(ident_b[:, :], ident[:, :]).then_inc(conv_nat_ready, 1)

            def statistics(n):
                dve.wait_ge(in_x[n], 16)
                for b in range(n * NB // X_CHUNKS, (n + 1) * NB // X_CHUNKS):
                    steps.did(dve.bn_stats(stats[:, b, :], x_all[:, b, :]))

            for n in range(X_CHUNKS // 2):
                statistics(n)
            dve.wait_ge(prep_out, 7)
            dve.wait_ge(in_misc, 16 * MISC_LOADS)
            dve.tensor_reduce(rmax[:, 2:3], pw1_f[:, :], AX, ALU.max, apply_absolute_value=True).then_inc(max_col, 1)
            statistics(4)
            dve.wait_ge(max_row, 1)
            dve.tensor_reduce(star[:, 2:3], bank[6][0:1, 128:256], AX, ALU.max).then_inc(star_ready, 1)
            statistics(5)
            dve.wait_ge(bcast_done, 1)
            steps.then(dve.tensor_copy(bcast[:, :], bank[6][:, 256:259]))
            steps.then(dve.tensor_scalar(bcast[:, 2:3], bcast[:, 2:3], 1e-30, None, ALU.max))
            dve.reciprocal(rmax[:, 2:3], bcast[:, 2:3]).then_inc(bcast_done, 1)
            dve.wait_ge(bcast_done, 2)
            steps.then(dve.tensor_scalar(pw1_f[:, :], pw1_f[:, :], rmax[:, 2:3], None, ALU.mult))
            steps.then(dve.tensor_copy(pw1_h[:, :], pw1_f[:, :]))
            tt(pw1_l[:, :], pw1_f[:, :], pw1_h[:, :], ALU.subtract).then_inc(pw1_parts, 1)
            dve.wait_ge(filt_done, 1)
            steps.did(dve.tensor_copy(f_res[:, 0:2, :], bank[5][:, 0:2 * NF].rearrange("p (a f) -> p a f", a=2)))
            steps.then(dve.tensor_copy(f_res[:, 2:4, :], sw_nat[:, :, :]))
            for part in range(3):
                steps.then(dve.tensor_copy(f_part[:, part, :, :], f_res[:, :, :]))
                if part < 2:
                    steps.then(tt(f_res[:, :, :], f_res[:, :, :], f_part[:, part, :, :], ALU.subtract))
            dve.wait_ge(zeroed, 2)
            for g in range(GROUPS):
                for branch in range(2):
                    sides = slice(2 * branch, 2 * branch + 2)
                    col = g * 8 + (1 - branch) * NF
                    dve.tensor_copy(f_cols[:, sides, col:col + NF], f_part[:, RIGHT_PART[g], sides, :]).then_inc(filt_cols, 1)
            statistics(6)
            statistics(7)

            steps.settle()
            m_e, m_o, v_e, v_o = stats[:, :, 1], stats[:, :, 4], stats[:, :, 2], stats[:, :, 5]
            t0, t1, t2, t3, t4, t5 = (small[:, n, :] for n in range(1, 7))
            steps.did(tt(t0, m_e, m_o, ALU.add))
            steps.did(tt(t1, m_e, m_o, ALU.subtract))
            steps.did(tt(t2, v_e, v_o, ALU.add))
            steps.settle()
            dve.tensor_scalar(mean[:, :], t0, 0.5, None, ALU.mult).then_inc(gm_in, 1)
            steps.then(dve.scalar_tensor_tensor(out=t3, in0=t1, scalar=0.25, in1=t1, op0=ALU.mult, op1=ALU.mult))
            steps.did(dve.scalar_tensor_tensor(out=var[:, :], in0=t2, scalar=1.0 / HW, in1=t3, op0=ALU.mult, op1=ALU.add))

            def group_norm(n, m, v, centred):
                dve.wait_ge(gm_out, n)
                steps.did(dve.tensor_copy(g_mean[:, :], bank[6][:, 64:64 + NB]))
                steps.then(tt(centred, m, bank[6][:, 64:64 + NB], ALU.subtract))
                steps.then(tt(t4, centred, centred, ALU.mult))
                tt(t5, t4, v, ALU.add).then_inc(gm_in, 1)
                dve.wait_ge(std_ready, n)
                steps.then(dve.reciprocal(small[:, 7, :], small[:, 0, :]))

            group_norm(1, mean[:, :], var[:, :], t0)
            steps.then(tt(t1, t0, small[:, 7, :], ALU.mult))
            steps.did(tt(nan_mask[:, :], t1, t1, ALU.is_equal))
            steps.then(dve.memset(t2, 0.0))
            steps.then(dve.copy_predicated(t2, nan_mask[:, :], t1))
            dve.tensor_scalar(k_in[:, 0, :], t2, FMAX, -FMAX, ALU.min, ALU.max).then_inc(kan_in, 1)
            dve.wait_ge(kan_in, 1)

            def kan_layer(layer, n, grid):
                s = k_in[0:n, 0, :].unsqueeze(1)
                knots = grid[:, :].unsqueeze(2)
                full = [n, KNOTS, NB]
                steps.did(tt(k_dist[0:n, :, :], s.broadcast_to(full), knots.broadcast_to(full), ALU.subtract))
                steps.did(tt(k_ge[0:n, :, :], s.broadcast_to(full), knots.broadcast_to(full), ALU.is_ge))
                steps.did(tt(k_lt[0:n, :, :], s.broadcast_to(full), knots.broadcast_to(full), ALU.is_lt))
                steps.settle()
                steps.then(tt(k_bas[0:n, :, :], k_ge[0:n, 0:KNOTS - 1, :], k_lt[0:n, 1:KNOTS, :], ALU.mult))
                for k in range(1, ORDER + 1):
                    m = KNOTS - k
                    steps.then(tt(k_m[0:n, 0:m, :], k_bas[0:n, 0:m, :],
                                  k_inv[0:n, layer, k - 1, 0:m].unsqueeze(2).broadcast_to([n, m, NB]), ALU.mult))
                    steps.did(tt(k_ge[0:n, 0:m - 1, :], k_dist[0:n, 0:m - 1, :], k_m[0:n, 0:m - 1, :], ALU.mult))
                    steps.then(tt(k_lt[0:n, 0:m - 1, :], k_dist[0:n, k + 1:KNOTS, :], k_m[0:n, 1:m, :], ALU.mult))
                    if k < ORDER:
                        steps.then(tt(k_bas[0:n, 0:m - 1, :], k_ge[0:n, 0:m - 1, :], k_lt[0:n, 0:m - 1, :], ALU.subtract))
                    else:
                        tt(k_rhs[0:n, 0:NK, :], k_ge[0:n, 0:NK, :], k_lt[0:n, 0:NK, :], ALU.subtract).then_inc(kan_rhs, 1)
                dve.wait_ge(kan_sig, 1 + 2 * layer)
                tt(k_rhs[0:n, NK, :], k_in[0:n, 0, :], k_in[0:n, 1, :], ALU.mult).then_inc(kan_rhs, 1)

            kan_layer(0, C, grid1_sb)
            dve.wait_ge(kan_sig, 2)
            tt(k_in[0:KH, 0, :], bank[7][0:KH, 0:NB], k_in[0:KH, 1, :], ALU.mult).then_inc(kan_in, 1)
            dve.wait_ge(kan_in, 2)
            kan_layer(1, KH, grid2_sb)
            dve.wait_ge(kan_sig, 4)

            ca, cb, cza, czb = (coef[:, n, :] for n in range(4))
            steps.then(tt(t1, k_in[:, 1, :], small[:, 7, :], ALU.mult))
            steps.did(dve.tensor_scalar(ca, t1, 1.0, None, ALU.add))
            steps.then(dve.scalar_tensor_tensor(out=cb, in0=g_mean[:, :], scalar=-1.0, in1=t1, op0=ALU.mult, op1=ALU.mult))
            steps.did(tt(t2, ca, mean[:, :], ALU.mult))
            steps.then(tt(t3, ca, ca, ALU.mult))
            steps.did(tt(var[:, :], t3, var[:, :], ALU.mult))
            tt(mean[:, :], t2, cb, ALU.add).then_inc(gm_in, 1)
            dve.wait_ge(gm_in, 3)
            steps.settle()
            group_norm(2, mean[:, :], var[:, :], t0)
            steps.did(tt(cza, ca, small[:, 7, :], ALU.mult))
            steps.then(tt(t1, cb, g_mean[:, :], ALU.subtract))
            steps.then(tt(czb, t1, small[:, 7, :], ALU.mult))
            dve.tensor_copy(eps[:, :], eps[:, :]).then_inc(coef_ready, 1)

            def z_low(it, u):
                base = it * IT
                for k in range(IT):
                    steps.did(dve.tensor_scalar(z32[:, k, :], one(x_all, base + k), one(cza.unsqueeze(2), base + k),
                                                one(czb.unsqueeze(2), base + k), ALU.mult, ALU.add))
                steps.settle()
                dve.wait_ge(zh_ready, base + IT)
                inner = zpad[u][:, :, :, 1:SIDE + 1, 1:SIDE + 1]
                z4 = z32[:, :, :].rearrange("p k (h w) -> p k h w", w=SIDE)
                tt(inner[:, 1], z4, inner[:, 0], ALU.subtract).then_inc(zl_ready, 1)
                for k in range(IT):
                    steps.did(dve.tensor_scalar(one(x_all, base + k), one(x_all, base + k), one(ca.unsqueeze(2), base + k),
                                                one(cb.unsqueeze(2), base + k), ALU.mult, ALU.add))
                steps.settle()
                dve.wait_ge(zl_ready, it + 1)
                kept = z_all[:, bass.ds(base, IT), :, :] if not isinstance(base, int) else z_all[:, base:base + IT, :, :]
                for part in range(2):
                    dve.tensor_copy(kept[:, :, part, :].rearrange("p k (h w) -> p k h w", w=SIDE),
                                    inner[:, part]).then_inc(z_kept, 1)

            def windows(it):
                dve.wait_ge(s1_ready, it + 1)
                flat = s1[:, :, :, :].rearrange("p j h w -> p (j h) w")
                mid = rows[:, 1, :, :].rearrange("p j h -> p (j h)")
                steps.then(dve.tensor_reduce(mid, flat, AX, ALU.add))
                steps.did(tt(rows[:, 0, :, :], rows[:, 1, :, :], s1[:, :, :, SIDE - 1], ALU.subtract))
                steps.then(tt(rows[:, 2, :, :], rows[:, 1, :, :], s1[:, :, :, 0], ALU.subtract))

                def at(ky):
                    w = win[:, ky]
                    return w[:, :, it, :] if isinstance(it, int) else w[:, :, bass.ds(it, 1), :].squeeze(2)
                steps.then(dve.tensor_reduce(at(1), rows[:, :, :, :], AX, ALU.add))
                steps.did(tt(at(0), at(1), rows[:, :, :, SIDE - 1], ALU.subtract))
                tt(at(2), at(1), rows[:, :, :, 0], ALU.subtract).then_inc(win_ready, 1)
                dve.wait_ge(win_ready, it + 1)
                steps.settle()
                dve.wait_ge(r2_ready, 2 * it + 2)
                dve.tensor_copy(one(r2_sum, it), r2_pair[:, :]).then_inc(r2_kept, 1)

            z_low(0, 0)
            z_low(1, 1)
            windows(0)
            start = steps.base + steps.n
            per = 2 * (2 * IT + 5)
            with dve.Fori(1, NIT // 2) as j:
                steps.enter(start - per, j, per)
                z_low(2 * j, 0)
                windows(2 * j - 1)
                z_low(2 * j + 1, 1)
                windows(2 * j)
            steps.leave(start, NIT // 2 - 1, per)
            windows(NIT - 1)

            dve.wait_ge(zeroed, 6)
            dve.wait_ge(r2_kept, NIT)
            win_b = win_p[:, :, :].rearrange("p q (n g j) -> p q n g j", g=2, j=2)
            taps = win[:, :, :, :, :].rearrange("p a b n j -> p (a b) n j")
            r2_b = r2_p[:, :].rearrange("p (n g j) -> p n g j", g=2, j=2)
            for g in range(2):
                rows_g = slice(HID * g, HID * g + HID)
                for u in range(2):
                    rows_u = slice(HID * u, HID * u + HID)
                    dve.tensor_scalar(win_b[rows_u, 0:4, :, g, :], taps[rows_g, u:8:2], 1.0 / HW, None, ALU.mult).then_inc(sums_ready, 1)
                dve.tensor_scalar(win_b[HID:P, 4, :, g, :], taps[rows_g, 8], 1.0 / HW, None, ALU.mult).then_inc(sums_ready, 1)
                dve.tensor_scalar(r2_b[:, :, g, :], r2_sum[rows_g, :, :], 1.0 / HW, None, ALU.mult).then_inc(sums_ready, 1)

            def halves(i):
                dve.wait_ge(sq_ready, i + 1)
                if not isinstance(i, int) or i >= 1:
                    dve.wait_ge(xt_done, i)
                dve.tensor_scalar(xp.rearrange("p t m -> p (t m)"), sq_v, bcast[:, 0:1],
                                  bcast[:, 1:2], ALU.mult, ALU.add).then_inc(xp_ready, 1)
                dve.wait_ge(xp_ready, i + 1)
                if not isinstance(i, int) or i >= 1:
                    dve.wait_ge(dft_done, i)
                    dve.wait_ge(eo_ready, i)
                steps.did(tt(eo[:, 0, :], xp[:, 0, :], xp[:, 1, :], ALU.add))
                steps.settle()
                tt(eo[:, 1, :], xp[:, 0, :], xp[:, 1, :], ALU.subtract).then_inc(eo_ready, 1)

            def terms(i):
                dve.wait_ge(spec_ready, i + 1)
                dve.wait_ge(w_done, i + 1)
                if not isinstance(i, int) or i >= 1:
                    dve.wait_ge(prod_ready, 2 * i)
                wide_shape = [P, 2, 2, P - 2]
                tt(t_re[:, :, :, 2:P], spec[:, :, :, 2:P], mixed_slot[:, :, 0, 2:P].unsqueeze(2).broadcast_to(wide_shape), ALU.mult).then_inc(terms_ready, 1)
                tt(t_im[:, :, :, 2:P], spec[:, :, :, 2:P], mixed_slot[:, :, 1, 2:P].unsqueeze(2).broadcast_to(wide_shape), ALU.mult).then_inc(terms_ready, 1)
                tt(t_re[:, :, :, 0:2], spec[:, :, :, 0:2], mixed_slot[:, :, :, 0:2], ALU.mult).then_inc(terms_ready, 1)

            def spatial(i):
                dve.wait_ge(sw_ready, i + 1)
                dve.wait_ge(xt_done, i + 1)
                if not isinstance(i, int) or i >= 1:
                    dve.wait_ge(sp_done, i)
                tt(qt[:, :, :], bank[2].rearrange("p (m s) -> p m s", m=2), swt[:, :, :], ALU.mult).then_inc(qt_ready, 1)

            def finish(i):
                dve.wait_ge(out_done, i + 1)
                tt(one(x_all, i), bank[6][:, 0:HW], one(x_all, i), ALU.add).then_inc(fin_ready, 1)

            halves(0)
            dve.wait_ge(logits_done, 1)
            steps.then(tt(logit, bank[7].rearrange("p (t b) -> p t b", b=NB),
                          bias_t.unsqueeze(2).broadcast_to([P, 16, NB]), ALU.add))
            by_filter = logit.rearrange("p (s f m) b -> p s f (m b)", s=2, f=NF)
            sm = rt_max[:, 0:2, :]
            over = [P, 2, NF, 2 * NB]
            steps.then(dve.tensor_reduce(sm, by_filter.rearrange("p s f q -> p s q f"), AX, ALU.max))
            tt(by_filter, by_filter, sm.unsqueeze(2).broadcast_to(over), ALU.subtract).then_inc(soft_in, 1)
            dve.wait_ge(soft_exp, 1)
            steps.then(dve.tensor_reduce(sm, by_filter.rearrange("p s f q -> p s q f"), AX, ALU.add))
            steps.then(dve.reciprocal(rt_max[:, 2:4, :], sm))
            steps.then(tt(by_filter, by_filter, rt_max[:, 2:4, :].unsqueeze(2).broadcast_to(over), ALU.mult))
            src = logit
            for part in range(3):
                g = LEFT_PART.index(part)
                own = rt_cols[:, :, :, g * 8:g * 8 + 8].rearrange("p b m c -> p c m b")
                src4 = src[:, :, :].rearrange("p (c m) b -> p c m b", m=2)
                if part < 2:
                    dve.tensor_copy(rt_part[part][:, :, :], src[:, :, :]).then_inc(rt_ready, 1)
                    dve.wait_ge(rt_ready, part + 1)
                    steps.did(dve.tensor_copy(own, rt_part[part][:, :, :].rearrange("p (c m) b -> p c m b", m=2)))
                    steps.then(tt(rt_res, src[:, :, :], rt_part[part][:, :, :], ALU.subtract))
                    src = rt_res
                else:
                    dve.tensor_copy(own, src4).then_inc(rt_ready, 1)
            for n in range(1, NIT, 2):
                dve.wait_ge(rt_done, n + 1)
                dve.tensor_copy(route[0:8 * GROUPS, n * IT:(n + 1) * IT, :, :].rearrange("p b m c -> p (b m c)"),
                                bank[6][0:8 * GROUPS].bitcast(BF16)).then_inc(rt_out[1], 1)
            terms(0)
            halves(1)
            spatial(0)

            def round_of(i):
                terms(i + 1)
                halves(i + 2)
                spatial(i + 1)
                finish(i)

            round_of(0)
            start = steps.base + steps.n
            with dve.Fori(1, NB - 2) as i:
                steps.enter(start - 1, i, 1)
                round_of(i)
            steps.leave(start, NB - 3, 1)
            terms(NB - 1)
            spatial(NB - 1)
            finish(NB - 2)
            finish(NB - 1)

        @block.tensor
        def _(pe):
            mm = pe.matmul

            def turn(dst, src, n):
                return pe.transpose(dst, src, ident[0:n, 0:n])

            prep = [0]

            def group_bank():
                n = prep[0]
                if n >= 4:
                    pe.wait_ge(prep_out, n - 3)
                return bank[n % 4]

            def group_end(ins):
                ins.then_inc(prep_done, 1)
                prep[0] += 1

            pe.wait_ge(in_const, 16 * CONST_LOADS)
            pe.wait_ge(conv_nat_ready, 3)
            taps = conv_nat[:, :].rearrange("o (i t) -> o t i", t=TAPS)
            b = group_bank()
            for t in range(8):
                last = turn(b[:, t * HID:(t + 1) * HID], taps[0:HID, t, :], HID)
            group_end(last)
            b = group_bank()
            turn(b[:, 0:HID], taps[0:HID, 8, :], HID)
            group_end(turn(b[:, HID:2 * HID], rw1_nat[0:HID, :], HID))
            pe.wait_ge(kan_nat_ready, 2)
            b = group_bank()
            for k in range(NK + 1):
                last = turn(b[:, k * KH:(k + 1) * KH], kan1_nat[:, k, :], KH)
            group_end(last)
            for ks in (range(0, 4), range(4, 8), range(8, 9)):
                b = group_bank()
                for k in ks:
                    last = turn(b[0:KH, (k - ks[0]) * C:(k - ks[0] + 1) * C], kan2_nat[:, k, :], P)
                group_end(last)
            pe.wait_ge(in_misc, 16 * MISC_LOADS)
            b = group_bank()
            for t in range(2):
                last = turn(b[:, t * P:(t + 1) * P], pw1_nat[:, t, :], P)
            group_end(last)
            pe.wait_ge(in_rwc, 32)
            b = group_bank()
            for t in range(2):
                turn(b[:, t * P:(t + 1) * P], pw2_nat[:, t * P:(t + 1) * P], P)
            turn(b[:, 256:384], rwc_nat[:, :], P)
            group_end(turn(b[:, 384:400], bias_nat[:, :], 16))
            for half in range(2):
                b = group_bank()
                for t in range(4):
                    last = turn(b[0:HID, t * P:(t + 1) * P], rwf_nat[:, 4 * half + t, :], P)
                group_end(last)
            assert prep[0] == PREP_ACT
            for part in range(2):
                for k in range(4):
                    u, c = divmod(k, 2)
                    last = mm(bank[5][:, part * NF:(part + 1) * NF], sym_sb[:, u, c, part * P:(part + 1) * P],
                              cw_sb[:, u, c:2 * NF:2], start=(k == 0), stop=(k == 3))
            last.then_inc(filt_done, 1)
            pe.wait_ge(max_col, 1)
            turn(bank[6][0:1, 128:256], rmax[:, 2:3], P).then_inc(max_row, 1)
            pe.wait_ge(star_ready, 1)
            pe.wait_ge(const_set, 2)
            mm(bank[6][:, 256:259], ones[:, :], star[:, :], start=True, stop=True).then_inc(bcast_done, 1)
            pe.wait_ge(filt_cols, 2 * GROUPS)
            for n in range(4):
                last = pe.transpose(bank[4].bitcast(BF16)[:, n * P:(n + 1) * P], f_cols[:, n, :], ident_b[:, :])
            last.then_inc(filt_done, 1)

            def group_means(n):
                pe.wait_ge(gm_in, 2 * n - 1)
                mm(bank[6][:, 64:64 + NB], group[:, :], mean[:, :], start=True, stop=True).then_inc(gm_out, 1)
                pe.wait_ge(gm_in, 2 * n)
                mm(bank[6][:, 0:NB], group[:, :], small[:, 6, :], start=True, stop=True).then_inc(var_ready, 1)

            group_means(1)
            for layer, (n, w, dst) in enumerate(((C, kan1_t, bank[7][0:KH, 0:NB]), (KH, kan2_t, bank[7][:, 64:64 + NB]))):
                for k in range(NK + 1):
                    if k in (0, NK):
                        pe.wait_ge(kan_rhs, 2 * layer + 1 + k // NK)
                    last = mm(dst, w[:, k, :], k_rhs[0:n, k, :], start=(k == 0), stop=(k == NK))
                last.then_inc(kan_done, 1)
            group_means(2)

            pe.wait_ge(conv_parts, 1)

            def branches(it, u):
                pe.wait_ge(zl_ready, it + 1)
                if not isinstance(it, int) or it >= 2:
                    pe.wait_ge(r1_ready, it - 1)
                    pe.wait_ge(s1_ready, it - 1)
                    pe.wait_ge(r2_ready, 2 * it - 2)
                passes = ((conv_h, 0), (conv_l, 0), (conv_h, 1))
                for n, (w, part) in enumerate(passes):
                    for g in range(2):
                        last = mm(bank[2 + u][HID * g:HID * g + HID, :], w[:, TAPS, :],
                                  zpad[u][:, part, 2 * g:2 * g + 2, 1:SIDE + 1, 1:SIDE + 1], start=(n == 0), stop=(n == 2))
                last.then_inc(rw1_done, 1)
                for n, (w, part) in enumerate(passes):
                    for t in range(TAPS):
                        dy, dx = divmod(t, 3)
                        for g in range(2):
                            last = mm(bank[u][HID * g:HID * g + HID, :], w[:, t, :],
                                      zpad[u][:, part, 2 * g:2 * g + 2, dy:dy + SIDE, dx:dx + SIDE],
                                      start=(n == 0 and t == 0), stop=(n == 2 and t == TAPS - 1))
                last.then_inc(conv_done, 1)
                pe.wait_ge(r1_ready, it + 1)
                mm(bank[5 + u], rwc_t, r1[:, :], start=True, stop=True).then_inc(rwc_done, 1)

            branches(0, 0)
            branches(1, 1)
            with pe.Fori(1, NIT // 2) as j:
                branches(2 * j, 0)
                branches(2 * j + 1, 1)

            def expand(i):
                if not isinstance(i, int) or i >= 1:
                    pe.wait_ge(relu_ready, i)
                z = one(z_all, i)
                for t in range(2):
                    cols = slice(t * P, (t + 1) * P)
                    for n, (part, w) in enumerate(((0, pw1_h), (1, pw1_h), (0, pw1_l))):
                        last = mm(bank[0][:, t * MED:(t + 1) * MED], z[:, part, cols], w[:, :], start=(n == 0), stop=(n == 2))
                last.then_inc(v_done, 1)

            def transform(i):
                pe.wait_ge(eo_ready, i + 1)
                if not isinstance(i, int) or i >= 1:
                    pe.wait_ge(spec_ready, i)
                dst = bank[1].rearrange("p (m a s) -> p m a s", m=2, a=2)
                for odd in range(2):
                    for m in range(2):
                        last = mm(dst[:, m, :, 64 * odd:64 * odd + 64], eo[:, odd, m * P:(m + 1) * P], forward[:, odd, :, :],
                                  start=True, stop=True)
                last.then_inc(dft_done, 1)
                if not isinstance(i, int) or i >= 1:
                    pe.wait_ge(qt_ready, i)
                for m in range(2):
                    for t in range(2):
                        last = turn(bank[2][:, m * HW + t * P:m * HW + (t + 1) * P], xp[:, t, m * P:(m + 1) * P], P)
                last.then_inc(xt_done, 1)

            def mix(i):
                if not isinstance(i, int) or i >= 1:
                    pe.wait_ge(terms_ready, 3 * i)
                    pe.wait_ge(sw_ready, i)
                r = one(route, i)
                for m in range(2):
                    for side in range(2):
                        last = mm(bank[3 + side][:, m * HW:(m + 1) * HW], r[:, m, :], filters[:, side * HW:(side + 1) * HW],
                                  start=True, stop=True)
                last.then_inc(w_done, 1)

            def reduce(i):
                pe.wait_ge(prod_ready, 2 * i + 2)
                if not isinstance(i, int) or i >= 1:
                    pe.wait_ge(y_ready, i)
                for part in range(2):
                    for m in range(2):
                        last = mm(bank[5][:, part * C:(part + 1) * C], prod[:, m, part, :], pw2_t[:, m, :],
                                  start=(m == 0), stop=(m == 1))
                last.then_inc(y_done, 1)

            def compose(i):
                pe.wait_ge(qt_ready, i + 1)
                if not isinstance(i, int) or i >= 1:
                    pe.wait_ge(fin_ready, i)
                for m in range(2):
                    last = mm(bank[6][:, 0:HW], pw2_t[:, m, :], qt[:, m, :], start=(m == 0), stop=False)
                last.then_inc(sp_done, 1)
                pe.wait_ge(y_ready, i + 1)
                for part in range(2):
                    last = mm(bank[6][:, 0:HW], y_sb[:, part, :], inverse[:, part, :], start=False, stop=(part == 1))
                last.then_inc(out_done, 1)

            pe.wait_ge(sp_ready, 8)
            pe.wait_ge(r2_ready, 2 * NIT)
            for n in range(SP_GROUPS):
                if n >= 2:
                    pe.wait_ge(prep_out, PREP_ACT + n - 1)
                for q in range(4):
                    t, p = divmod(4 * n + q, PAIRS)
                    k = pair_tap(p)
                    last = turn(bank[5 + n % 2][:, q * P:(q + 1) * P], sp_perm[:, t, k:k + 2, :].rearrange("o k i -> o (k i)"), P)
                last.then_inc(prep_done, 1)
            pe.wait_ge(z_kept, 2 * NIT)
            pe.wait_ge(pw1_parts, 1)
            expand(0)
            pe.wait_ge(prep_out, PREP_ACT + SP_GROUPS)
            pe.wait_ge(sums_ready, 8)
            for t in range(8):
                mm(bank[7][:, 256 + t * NB:256 + (t + 1) * NB], rwf_t[:, t, :], r2_p[:, :], start=True, stop=True)
            for t in range(8):
                for p in range(PAIRS):
                    last = mm(bank[7][:, t * NB:(t + 1) * NB], sp_t[:, t, p, :], win_p[:, p, :], start=(p == 0), stop=(p == PAIRS - 1))
            last.then_inc(logits_done, 1)
            transform(0)
            expand(1)
            pe.wait_ge(rt_ready, 3)
            pe.wait_ge(rt_dup, 3)
            for n in range(NIT):
                if n >= 2:
                    pe.wait_ge(rt_out[n % 2], n // 2)
                for k in range(IT):
                    for m in range(2):
                        last = pe.transpose(bank[5 + n % 2].bitcast(BF16)[0:8 * GROUPS, (2 * k + m) * P:(2 * k + m + 1) * P],
                                            rt_cols[:, n * IT + k, m, :], ident_b[:, :])
                last.then_inc(rt_done, 1)
            pe.wait_ge(rt_out[0], NIT // 2)
            pe.wait_ge(rt_out[1], NIT // 2)
            pe.wait_ge(filt_ready, 1)
            mix(0)

            def round_of(i):
                expand(i + 2)
                transform(i + 1)
                mix(i + 1)
                reduce(i)
                compose(i)

            round_of(0)
            with pe.Fori(1, NB - 2) as i:
                round_of(i)
            transform(NB - 1)
            mix(NB - 1)
            reduce(NB - 2)
            compose(NB - 2)
            reduce(NB - 1)
            compose(NB - 1)


NAMES = ["x", "L0_conv_grid1", "L0_conv_base_w1", "L0_conv_spline_w1", "L0_conv_scaler1", "L0_conv_grid2",
         "L0_conv_base_w2", "L0_conv_spline_w2", "L0_conv_scaler2", "L1_conv_w_pw1", "L1_conv_w_pw2",
         "L1_conv_star_scale", "L1_conv_star_bias", "L1_conv_rw_fc1_w", "L1_conv_rw_fc1_b", "L1_conv_rw_conv_w",
         "L1_conv_rw_conv_b", "L1_conv_rw_fc2_w", "L1_conv_rw_fc2_b", "L1_conv_sp_fc1_w", "L1_conv_sp_fc1_b",
         "L1_conv_sp_fc2_w", "L1_conv_sp_fc2_b", "L1_conv_complex_weights", "L1_conv_spatial_weights"]


def kernel(**inputs):
    import concourse.bacc as bacc
    from concourse.bass_utils import run_bass_kernel_spmd

    nc = bacc.Bacc("TRN2", target_bir_lowering=False, num_devices=1)
    arrays, args = {}, []
    given = [(name, np.ascontiguousarray(inputs[name])) for name in NAMES]
    given += [(f"const_{name}", a.astype(np.float32)) for name, a in constants().items()]
    for name, a in given:
        arrays[f"in_{name}"] = a
        args.append(nc.dram_tensor(f"in_{name}", a.shape, mybir.dt.from_np(a.dtype), kind="ExternalInput").ap())
    args.append(nc.dram_tensor("out_0", (NB, C, SIDE, SIDE), F32, kind="ExternalOutput").ap())
    build(nc, *args)
    r = run_bass_kernel_spmd(nc, [arrays], core_ids=[0])
    return r.results[0]["out_0"]
```

```python
from contextlib import ExitStack

import numpy as np

import concourse.bass as bass
from concourse import mybir

F32 = mybir.dt.float32
F16 = mybir.dt.float16
BF16 = mybir.dt.bfloat16
I32 = mybir.dt.int32
ALU = mybir.AluOpType
ACT = mybir.ActivationFunctionType
AX = mybir.AxisListType.X

P = 128
NB = 32
C = 128
SIDE = 16
HW = SIDE * SIDE
MED = 2 * C
NF = 4
HID = 64
TAPS = 9
PAD = SIDE + 2
KH = 16
KNOTS = 12
ORDER = 3
NK = KNOTS - 1 - ORDER
GROUP = 4
EPS = 1e-5
FMAX = 3.4028235e38

IT = 4
NIT = NB // IT
PAIRS = 5
GROUPS = 6
LEFT_PART = [0, 0, 0, 1, 1, 2]
RIGHT_PART = [0, 1, 2, 0, 1, 0]
X_CHUNKS = 8


def pair_tap(p):
    return min(2 * p, TAPS - 2)


def slots():
    inner = range(1, SIDE // 2)
    half = SIDE // 2
    found = [((0, 0), (0, half)), ((half, 0), (half, half))]
    for first in (0, 1):
        for ky in range(first, SIDE, 2):
            found += [((ky, kx), (ky, kx)) for kx in inner]
        for ky in range(first, half, 2):
            if ky:
                found += [((ky, kx), (ky, kx)) for kx in (0, half)]
    assert len(found) == P
    return found


def constants():
    half = SIDE // 2
    fs = half + 1
    ident = np.eye(P)
    group = np.kron(np.eye(P // GROUP), np.full((GROUP, GROUP), 1.0 / GROUP))
    h, w = np.divmod(np.arange(HW), SIDE)
    forward = np.zeros((P, 2, 2, 64))
    inverse = np.zeros((P, 2, HW))
    sym = np.zeros((SIDE, fs, 2, 2, P))
    for n, (fa, fb) in enumerate(slots()):
        odd, col = divmod(n, 64)
        real = fa != fb
        for part, (ky, kx) in enumerate((fa, fb)):
            angle = 2 * np.pi * (ky * h + kx * w) / SIDE
            wave = np.cos(angle) if real or part == 0 else -np.sin(angle)
            forward[:, odd, part, col] = wave[:P] / SIDE
            inverse[n, part] = wave * (1 if real else 2) / SIDE
            re_im = 0 if real else part
            if real or kx not in (0, half):
                sym[ky, kx, re_im, part, n] = 1
            else:
                sym[ky, kx, re_im, part, n] = 0.5
                sym[(SIDE - ky) % SIDE, kx, re_im, part, n] = 0.5 if re_im == 0 else -0.5
    sym = sym.reshape(2, SIDE * fs // 2, 2, 2 * P).transpose(1, 0, 2, 3).reshape(SIDE * fs // 2, -1)
    return {
        "ident": ident, "group": group, "forward": forward.reshape(P, -1),
        "inverse": inverse.reshape(P, -1), "sym": sym,
    }


class Steps:

    def __init__(self, eng, sem):
        self.eng, self.sem, self.base, self.n = eng, sem, 0, 0

    def did(self, ins):
        ins.then_inc(self.sem, 1)
        self.n += 1

    def settle(self):
        self.eng.wait_ge(self.sem, self.base + self.n)

    def then(self, ins):
        self.did(ins)
        self.settle()

    def enter(self, start, i, per):
        self.base, self.n = start + i * per, 0

    def leave(self, start, rounds, per):
        assert self.n == per, self.n
        self.base, self.n = start + rounds * per, 0


EARLY = {"ident": P, "group": P, "grid1": KNOTS, "spline1": NK * KH, "base1": KH, "scaler1": KH}
KAN2 = {"grid2": KNOTS, "spline2": NK * C, "base2": C, "scaler2": C}
LATER = {"conv": TAPS * HID, "rw1": HID, "pw1": MED, "rwc": P, "pw2": MED, "logit_bias": 16, "hidden_bias": 3,
         "star": 2, "forward": 4 * 64, "inverse": 2 * HW, "pixel_filters": 2 * NF}
SYM = {"sym": 4 * 2 * P, "filters": 2 * 2 * NF}


def columns(pack, name):
    lo = sum(list(pack.values())[:list(pack).index(name)])
    return slice(lo, lo + pack[name])


def build(nc, x, early, kan2, later, sym, branch_r, branch_s, out):
    ctx = ExitStack()
    with ctx:
        def sb(name, shape, dt=F32):
            return ctx.enter_context(nc.sbuf_tensor(name, shape, dt))

        def ps(name, shape, dt=F32):
            return ctx.enter_context(nc.psum_tensor(name, shape, dt))

        def sem(name):
            return ctx.enter_context(nc.semaphore(name))

        x_all = sb("x_all", [P, NB, HW])
        z_all = sb("z_all", [P, NB, 2, HW], F16)
        early_sb = sb("early_sb", [P, sum(EARLY.values())])
        kan2_sb = sb("kan2_sb", [KH, sum(KAN2.values())])
        later_sb = sb("later_sb", [P, sum(LATER.values())])
        sym_all = sb("sym_all", [72, sum(SYM.values())])

        def of(tensor, pack, name):
            return tensor[:, columns(pack, name)]

        ident, group = of(early_sb, EARLY, "ident"), of(early_sb, EARLY, "group")
        grid1_sb, grid2_sb = of(early_sb, EARLY, "grid1"), of(kan2_sb, KAN2, "grid2")
        kan1_t = early_sb[:, columns(EARLY, "spline1").start:columns(EARLY, "base1").stop].rearrange("c (k o) -> c k o", o=KH)
        kan2_t = kan2_sb[:, columns(KAN2, "spline2").start:columns(KAN2, "base2").stop].rearrange("c (k o) -> c k o", o=C)
        scaler1_sb, scaler2_sb = of(early_sb, EARLY, "scaler1"), of(kan2_sb, KAN2, "scaler2")
        rwc_t = of(later_sb, LATER, "rwc")
        pw2_t = of(later_sb, LATER, "pw2").rearrange("m (t d) -> m t d", t=2)
        bias_t, bias_col = of(later_sb, LATER, "logit_bias"), of(later_sb, LATER, "hidden_bias")
        star = of(later_sb, LATER, "star")
        forward = of(later_sb, LATER, "forward").rearrange("p (a b c) -> p a b c", a=2, b=2)
        inverse = of(later_sb, LATER, "inverse").rearrange("p (a s) -> p a s", a=2)
        sw_nat = of(later_sb, LATER, "pixel_filters").rearrange("p (u f) -> p u f", u=2)
        sym_sb = of(sym_all, SYM, "sym").rearrange("p (u c s) -> p u c s", u=2, c=2)
        cw_sb = of(sym_all, SYM, "filters").rearrange("p (u f) -> p u f", u=2)
        split_cols = TAPS * HID + HID + MED
        split_src = later_sb[:, 0:split_cols]
        spans = [columns(LATER, name) for name in ("conv", "rw1", "pw1")]
        split_h = sb("split_h", [P, split_cols], F16)
        split_l = sb("split_l", [P, split_cols], F16)
        conv_h, conv_l = (w[:, 0:(TAPS + 1) * HID].rearrange("p (t o) -> p t o", o=HID) for w in (split_h, split_l))
        pw1_h, pw1_l = (w[:, spans[2]] for w in (split_h, split_l))
        maxima = sb("maxima", [P, 3])
        maxima_t = sb("maxima_t", [3, P])
        maxima_d = sb("maxima_d", [3, 3])
        w_max = sb("w_max", [P, 3])
        w_inv = sb("w_inv", [P, 3])
        ones = sb("ones", [3, P])
        ident_b = sb("ident_b", [P, P], BF16)
        coef = sb("coef", [P, 4, NB])
        eps = sb("eps", [P, 1])
        filters = sb("filters", [P, 512], BF16)
        rwf_t = sb("rwf_t", [HID, 8, P])
        sp_t = sb("sp_t", [P, 8, PAIRS, P])
        stats = sb("stats", [P, NB, 6])
        mean = sb("mean", [P, NB])
        var = sb("var", [P, NB])
        g_mean = sb("g_mean", [P, NB])
        small = sb("small", [P, 8, NB])
        nan_mask = sb("nan_mask", [P, NB], I32)
        k_inv = sb("k_inv", [P, 2, ORDER, KNOTS - 1])
        k_den = sb("k_den", [P, 2, ORDER, KNOTS - 1])
        k_in = sb("k_in", [P, 3, NB])
        k_dist = sb("k_dist", [P, KNOTS, NB])
        k_ge = sb("k_ge", [P, KNOTS, NB])
        k_rel = sb("k_rel", [P, ORDER, KNOTS - 1, NB])
        k_bas = sb("k_bas", [P, KNOTS - 1, NB])
        k_t = sb("k_t", [P, KNOTS - 1, NB])
        k_u = sb("k_u", [P, KNOTS - 1, NB])
        k_rhs = sb("k_rhs", [P, NK + 1, NB])
        zpads = sb("zpads", [P, 2, 2, IT, PAD, PAD], F16)
        zpad = [zpads[:, u] for u in range(2)]
        z32 = sb("z32", [P, IT, HW])
        r1 = sb("r1", [P, 512])
        s1 = sb("s1", [P, 2, SIDE, SIDE])
        r2 = sb("r2", [P, 2, HW], BF16)
        r2_pair = sb("r2_pair", [P, 2])
        r2_sum = sb("r2_sum", [P, NIT, 2])
        rows = sb("rows", [P, 3, 2, SIDE])
        win = sb("win", [P, 3, 3, NIT, 2])
        win_p = sb("win_p", [P, PAIRS, NB])
        r2_p = sb("r2_p", [HID, NB])
        rt_max = sb("rt_max", [P, 4, 2 * NB])
        rt_part = [sb(f"rt_part{n}", [P, 2 * 8, NB], BF16) for n in range(2)]
        route = sb("route", [P, NB, 2, P], BF16)
        f_cols = sb("f_cols", [P, 4, P], BF16)
        f_res = sb("f_res", [P, 4, NF])
        f_part = sb("f_part", [P, 3, 4, NF], BF16)
        logit = sb("logit", [P, 16, NB])[:, :, :]
        rt_res = sb("rt_res", [P, 16, NB])[:, :, :]
        rt_cols = sb("rt_cols", [P, NB, 2, 8 * GROUPS], BF16)[:, :, :, :]
        relu_v, sq_v = (sb(name, [P, 512])[:, :] for name in ("relu_v", "sq_v"))
        xp, eo, swt, qt = (sb(name, [P, 2, 256])[:, :, :] for name in ("xp", "eo", "swt", "qt"))
        spec, t_re, prod = (sb(name, [P, 2, 2, P])[:, :, :, :] for name in ("spec", "t_re", "prod"))
        t_im = sb("t_im", [P, 2, 2, P])
        y_sb = sb("y_sb", [P, 2, C])

        bank = [ps(f"bank{n}", [P, 512])[:, :] for n in range(8)]
        mixed_slot = bank[3].rearrange("p (m a s) -> p m a s", m=2, a=2)
        mixed_pixel = bank[4].rearrange("p (m s) -> p m s", m=2)

        in_x = [sem(f"in_x{n}") for n in range(X_CHUNKS)]
        in_early, in_kan2, in_later, in_sym, in_branch = (sem(n) for n in (
            "in_early", "in_kan2", "in_later", "in_sym", "in_branch"))
        zeroed, const_set, kan_w_ready, inv_ready = (sem(n) for n in ("zeroed", "const_set", "kan_w_ready", "inv_ready"))
        dve_step, pool_step = sem("dve_step"), sem("pool_step")
        max_cols, max_rows, max_diag, max_done, max_ready = (sem(n) for n in (
            "max_cols", "max_rows", "max_diag", "max_done", "max_ready"))
        scaled, split_hi, split_lo = sem("scaled"), sem("split_hi"), sem("split_lo")
        filt_done, filt_copied, filt_cols, filt_ready = (sem(n) for n in ("filt_done", "filt_copied", "filt_cols", "filt_ready"))
        dist_ready, rel_ready = sem("dist_ready"), sem("rel_ready")
        gm_in, gm_out = sem("gm_in"), sem("gm_out")
        var_ready, std_ready = sem("var_ready"), sem("std_ready")
        kan_in, kan_sig, kan_rhs, kan_done = sem("kan_in"), sem("kan_sig"), sem("kan_rhs"), sem("kan_done")
        coef_ready = sem("coef_ready")
        zh_ready, zl_ready, z_kept = sem("zh_ready"), sem("zl_ready"), sem("z_kept")
        rw1_done, conv_done, rwc_done = sem("rw1_done"), sem("conv_done"), sem("rwc_done")
        r1_ready, s1_ready, r2_ready = sem("r1_ready"), sem("s1_ready"), sem("r2_ready")
        r2_kept, win_ready = sem("r2_kept"), sem("win_ready")
        sums_ready, logits_done, soft_in, soft_exp = (sem(n) for n in ("sums_ready", "logits_done", "soft_in", "soft_exp"))
        rt_ready, rt_dup, rt_done = sem("rt_ready"), sem("rt_dup"), sem("rt_done")
        rt_out = [sem("rt_out_act"), sem("rt_out_dve")]
        v_done, relu_ready, sq_ready, xp_ready, eo_ready = (sem(n) for n in (
            "v_done", "relu_ready", "sq_ready", "xp_ready", "eo_ready"))
        dft_done, xt_done, w_done, spec_ready, sw_ready = (sem(n) for n in (
            "dft_done", "xt_done", "w_done", "spec_ready", "sw_ready"))
        terms_ready, prod_ready, qt_ready, y_done, y_ready = (sem(n) for n in (
            "terms_ready", "prod_ready", "qt_ready", "y_done", "y_ready"))
        sp_done, out_done, fin_ready, stored = (sem(n) for n in ("sp_done", "out_done", "fin_ready", "stored"))

        def one(ap, n):
            if isinstance(n, int):
                return ap[:, n]
            return ap[:, bass.ds(n, 1)].squeeze(1)

        block = ctx.enter_context(nc.Block())

        @block.sync
        def _(sp):
            k = NB // X_CHUNKS

            def load(n):
                sp.dma_start(x_all[:, n * k:(n + 1) * k, :],
                             x[n * k:(n + 1) * k].rearrange("b c h w -> c b (h w)")).then_inc(in_x[n], 16)

            sp.dma_start(early_sb[:, :], early).then_inc(in_early, 16)
            for n in range(6):
                load(n)
            sp.dma_start(later_sb[:, :], later).then_inc(in_later, 16)
            for n in range(6, X_CHUNKS):
                load(n)
            sp.dma_start(rwf_t[:, :, :], branch_r.rearrange("i (t o) -> i t o", o=P)).then_inc(in_branch, 16)
            sp.dma_start(sp_t[:, :, :, :], branch_s.rearrange("i (t q o) -> i t q o", t=8, q=PAIRS)).then_inc(in_branch, 16)
            out_v = out.rearrange("b c h w -> c b (h w)")
            with sp.Fori(0, NB) as i:
                sp.wait_ge(fin_ready, i + 1)
                sp.dma_start(one(out_v, i), one(x_all, i)).then_inc(stored, 16)
            sp.wait_ge(stored, 16 * NB)

        @block.gpsimd
        def _(pool):
            steps = Steps(pool, pool_step)
            pool.memset(f_cols[:, :, :], 0.0).then_inc(zeroed, 1)
            pool.memset(zpads[:, :, :, :, :, :], 0.0).then_inc(zeroed, 1)
            pool.memset(win_p[:, PAIRS - 1, :], 0.0).then_inc(zeroed, 1)
            pool.memset(t_im[:, :, :, :], 0.0).then_inc(zeroed, 1)
            pool.wait_ge(in_kan2, 16)
            pool.tensor_tensor(kan2_t[:, 0:NK, :], kan2_t[:, 0:NK, :],
                               scaler2_sb.unsqueeze(1).broadcast_to([KH, NK, C]), ALU.mult).then_inc(kan_w_ready, 1)
            pool.memset(route[:, :, :, :], 0.0).then_inc(zeroed, 1)
            pool.wait_ge(filt_copied, 1)
            pool.wait_ge(in_later, 16)
            steps.then(pool.tensor_copy(f_res[:, 2:4, :], sw_nat))
            for part in range(3):
                steps.then(pool.tensor_copy(f_part[:, part, :, :], f_res[:, :, :]))
                if part < 2:
                    steps.then(pool.tensor_tensor(f_res[:, :, :], f_res[:, :, :], f_part[:, part, :, :], ALU.subtract))
            pool.wait_ge(zeroed, 1)
            for g in range(GROUPS):
                for branch in range(2):
                    sides = slice(2 * branch, 2 * branch + 2)
                    col = g * 8 + (1 - branch) * NF
                    pool.tensor_copy(f_cols[:, sides, col:col + NF], f_part[:, RIGHT_PART[g], sides, :]).then_inc(filt_cols, 1)
            pool.wait_ge(split_hi, 1)
            pool.tensor_tensor(split_l[:, :], split_src, split_h[:, :], ALU.subtract).then_inc(split_lo, 1)

            def places(layer, n):
                pool.wait_ge(inv_ready, 2)
                pool.wait_ge(dist_ready, layer + 1)
                for k in range(1, ORDER + 1):
                    m = KNOTS - k
                    pool.tensor_tensor(k_rel[0:n, k - 1, 0:m, :], k_dist[0:n, 0:m, :],
                                       k_inv[0:n, layer, k - 1, 0:m].unsqueeze(2).broadcast_to([n, m, NB]), ALU.mult).then_inc(rel_ready, 1)

            places(0, C)
            places(1, KH)

            def products(i):
                pool.wait_ge(terms_ready, 3 * i + 3)
                if not isinstance(i, int) or i >= 1:
                    pool.wait_ge(y_done, i)
                pool.tensor_tensor(prod[:, :, 0, :], t_re[:, :, 0, :], t_im[:, :, 1, :], ALU.subtract).then_inc(prod_ready, 1)
                pool.tensor_tensor(prod[:, :, 1, :], t_re[:, :, 1, :], t_im[:, :, 0, :], ALU.add).then_inc(prod_ready, 1)

            products(0)
            with pool.Fori(1, NB - 1) as i:
                products(i)
            products(NB - 1)

        @block.scalar
        def _(act):
            act.dma_start(kan2_sb[:, :], kan2).then_inc(in_kan2, 16)
            act.dma_start(sym_all[:, :], sym).then_inc(in_sym, 16)
            act.wait_ge(filt_done, 1)
            act.activation(f_res[:, 0:2, :], bank[5][:, 0:2 * NF].rearrange("p (a f) -> p a f", a=2), ACT.Identity).then_inc(filt_copied, 1)
            act.wait_ge(max_ready, 1)
            for n, span in enumerate(spans):
                act.activation(later_sb[:, span], later_sb[:, span], ACT.Identity, scale=w_inv[:, n:n + 1]).then_inc(scaled, 1)
            act.wait_ge(scaled, 3)
            act.activation(split_h[:, :], split_src, ACT.Identity).then_inc(split_hi, 1)
            act.wait_ge(filt_done, 2)
            act.activation(filters[:, :], bank[4].bitcast(BF16)[:, 0:512], ACT.Identity).then_inc(filt_ready, 1)

            act.wait_ge(const_set, 1)
            act.wait_ge(var_ready, 1)
            act.activation(small[:, 0, :], bank[6][:, 0:NB], ACT.Sqrt, bias=eps[:, 0:1]).then_inc(std_ready, 1)
            act.wait_ge(kan_in, 1)
            act.activation(k_in[:, 1, :], k_in[:, 0, :], ACT.Sigmoid).then_inc(kan_sig, 1)
            act.wait_ge(kan_done, 1)
            act.activation(k_in[0:KH, 1, :], bank[7][0:KH, 0:NB], ACT.Sigmoid).then_inc(kan_sig, 1)
            act.wait_ge(kan_in, 2)
            act.activation(k_in[0:KH, 1, :], k_in[0:KH, 0, :], ACT.Sigmoid).then_inc(kan_sig, 1)
            act.wait_ge(kan_done, 2)
            act.activation(k_in[:, 1, :], bank[7][:, 64:64 + NB], ACT.Sigmoid).then_inc(kan_sig, 1)
            act.wait_ge(var_ready, 2)
            act.activation(small[:, 0, :], bank[6][:, 0:NB], ACT.Sqrt, bias=eps[:, 0:1]).then_inc(std_ready, 1)

            def z_high(it, u):
                if not isinstance(it, int) or it >= 2:
                    act.wait_ge(conv_done, it - 1)
                    act.wait_ge(rw1_done, it - 1)
                    act.wait_ge(z_kept, 2 * it - 2)
                for k in range(IT):
                    b = it * IT + k
                    act.activation(zpad[u][:, 0, k, 1:SIDE + 1, 1:SIDE + 1],
                                   one(x_all, b).rearrange("p (h w) -> p h w", w=SIDE), ACT.Identity,
                                   bias=one(coef[:, 3, :].unsqueeze(2), b),
                                   scale=one(coef[:, 2, :].unsqueeze(2), b)).then_inc(zh_ready, 1)

            def hidden(it, u):
                act.wait_ge(rw1_done, it + 1)
                if not isinstance(it, int) or it >= 1:
                    act.wait_ge(rwc_done, it)
                act.activation(r1[:, :], bank[2 + u], ACT.Relu, bias=bias_col[:, 1:2], scale=w_max[:, 1:2]).then_inc(r1_ready, 1)
                act.wait_ge(conv_done, it + 1)
                if not isinstance(it, int) or it >= 1:
                    act.wait_ge(win_ready, it)
                    act.wait_ge(r2_kept, it)
                act.activation(s1[:, :, :, :].rearrange("p j h w -> p (j h w)"), bank[u], ACT.Relu,
                               bias=bias_col[:, 0:1], scale=w_max[:, 0:1]).then_inc(s1_ready, 1)
                act.wait_ge(rwc_done, it + 1)
                if not isinstance(it, int) or it >= 1:
                    act.wait_ge(r2_ready, 2 * it)
                for j in range(2):
                    act.activation(r2[:, j, :], bank[5 + u][:, j * HW:(j + 1) * HW], ACT.Relu,
                                   bias=bias_col[:, 2:3], accum_out=r2_pair[:, j:j + 1]).then_inc(r2_ready, 1)

            act.wait_ge(zeroed, 2)
            act.wait_ge(coef_ready, 1)
            z_high(0, 0)
            z_high(1, 1)
            hidden(0, 0)
            with act.Fori(1, NIT // 2) as j:
                z_high(2 * j, 0)
                hidden(2 * j - 1, 1)
                z_high(2 * j + 1, 1)
                hidden(2 * j, 0)
            hidden(NIT - 1, 1)

            def relu_square(i):
                act.wait_ge(v_done, i + 1)
                if not isinstance(i, int) or i >= 1:
                    act.wait_ge(sq_ready, i)
                act.activation(relu_v[:, :], bank[0], ACT.Relu, scale=w_max[:, 2:3]).then_inc(relu_ready, 1)
                act.wait_ge(relu_ready, i + 1)
                if not isinstance(i, int) or i >= 1:
                    act.wait_ge(xp_ready, i)
                act.activation(sq_v[:, :], relu_v[:, :], ACT.Square).then_inc(sq_ready, 1)

            def spectrum(i):
                act.wait_ge(dft_done, i + 1)
                if not isinstance(i, int) or i >= 1:
                    act.wait_ge(terms_ready, 3 * i)
                act.activation(spec[:, :, :, :].rearrange("p m a s -> p (m a s)"), bank[1], ACT.Identity).then_inc(spec_ready, 1)

            def spatial_mix(i):
                act.wait_ge(w_done, i + 1)
                if not isinstance(i, int) or i >= 1:
                    act.wait_ge(qt_ready, i)
                act.activation(swt[:, :, :], mixed_pixel, ACT.Identity).then_inc(sw_ready, 1)

            def y_copy(i):
                act.wait_ge(y_done, i + 1)
                if not isinstance(i, int) or i >= 1:
                    act.wait_ge(out_done, i)
                act.activation(y_sb[:, :, :].rearrange("p a d -> p (a d)"), bank[5][:, 0:2 * C], ACT.Identity).then_inc(y_ready, 1)

            relu_square(0)
            spectrum(0)
            act.wait_ge(soft_in, 1)
            act.activation(logit, logit, ACT.Exp).then_inc(soft_exp, 1)
            relu_square(1)
            copies = 0
            for g in range(GROUPS):
                part = LEFT_PART[g]
                if g in (0, 3, 5):
                    continue
                act.wait_ge(rt_ready, part + 1)
                act.activation(rt_cols[:, :, :, g * 8:g * 8 + 8].rearrange("p b m c -> p c m b"),
                               rt_part[part][:, :, :].rearrange("p (c m) b -> p c m b", m=2), ACT.Identity).then_inc(rt_dup, 1)
                copies += 1
            assert copies == 3
            for n in range(0, NIT, 2):
                act.wait_ge(rt_done, n + 1)
                act.activation(route[0:8 * GROUPS, n * IT:(n + 1) * IT, :, :].rearrange("p b m c -> p (b m c)"),
                               bank[5][0:8 * GROUPS].bitcast(BF16), ACT.Identity).then_inc(rt_out[0], 1)
            spatial_mix(0)

            def round_of(i):
                relu_square(i + 2)
                spectrum(i + 1)
                spatial_mix(i + 1)
                y_copy(i)

            round_of(0)
            with act.Fori(1, NB - 2) as i:
                round_of(i)
            spectrum(NB - 1)
            spatial_mix(NB - 1)
            y_copy(NB - 2)
            y_copy(NB - 1)

        @block.vector
        def _(dve):
            steps = Steps(dve, dve_step)
            tt = dve.tensor_tensor

            dve.memset(eps[:, :], EPS).then_inc(const_set, 1)
            dve.memset(ones[:, :], 1.0).then_inc(const_set, 1)
            dve.wait_ge(in_early, 16)
            tt(kan1_t[:, 0:NK, :], kan1_t[:, 0:NK, :],
               scaler1_sb.unsqueeze(1).broadcast_to([C, NK, KH]), ALU.mult).then_inc(kan_w_ready, 1)
            dve.tensor_copy(ident_b[:, :], ident).then_inc(const_set, 1)

            def inverses(layer, n, grid):
                for k in range(1, ORDER + 1):
                    steps.did(tt(k_den[0:n, layer, k - 1, 0:KNOTS - k], grid[:, k:KNOTS], grid[:, 0:KNOTS - k], ALU.subtract))
                steps.settle()
                for k in range(1, ORDER + 1):
                    last = dve.reciprocal(k_inv[0:n, layer, k - 1, 0:KNOTS - k], k_den[0:n, layer, k - 1, 0:KNOTS - k])
                    if k < ORDER:
                        steps.did(last)
                last.then_inc(inv_ready, 1)

            inverses(0, C, grid1_sb)
            dve.wait_ge(in_kan2, 16)
            inverses(1, KH, grid2_sb)

            def statistics(n):
                dve.wait_ge(in_x[n], 16)
                for b in range(n * NB // X_CHUNKS, (n + 1) * NB // X_CHUNKS):
                    steps.did(dve.bn_stats(stats[:, b, :], x_all[:, b, :]))

            for n in range(6):
                statistics(n)
            dve.wait_ge(in_later, 16)
            for n, span in enumerate(spans):
                dve.tensor_reduce(maxima[:, n:n + 1], later_sb[:, span], AX, ALU.max, apply_absolute_value=True).then_inc(max_cols, 1)
            statistics(6)
            dve.wait_ge(max_rows, 1)
            steps.then(dve.tensor_reduce(maxima_t[:, 0:1], bank[6][0:3, 128:256], AX, ALU.max))
            dve.tensor_scalar(maxima_d[:, :], ident[0:3, 0:3], maxima_t[:, 0:1], None, ALU.mult).then_inc(max_diag, 1)
            statistics(7)
            dve.wait_ge(max_done, 1)
            steps.then(dve.tensor_scalar(w_max[:, :], bank[6][:, 256:259], 1e-30, None, ALU.max))
            dve.reciprocal(w_inv[:, :], w_max[:, :]).then_inc(max_ready, 1)

            steps.settle()
            m_e, m_o, v_e, v_o = stats[:, :, 1], stats[:, :, 4], stats[:, :, 2], stats[:, :, 5]
            t0, t1, t2, t3, t4, t5 = (small[:, n, :] for n in range(1, 7))
            steps.did(tt(t0, m_e, m_o, ALU.add))
            steps.did(tt(t1, m_e, m_o, ALU.subtract))
            steps.did(tt(t2, v_e, v_o, ALU.add))
            steps.settle()
            dve.tensor_scalar(mean[:, :], t0, 0.5, None, ALU.mult).then_inc(gm_in, 1)
            steps.then(dve.scalar_tensor_tensor(out=t3, in0=t1, scalar=0.25, in1=t1, op0=ALU.mult, op1=ALU.mult))
            steps.did(dve.scalar_tensor_tensor(out=var[:, :], in0=t2, scalar=1.0 / HW, in1=t3, op0=ALU.mult, op1=ALU.add))

            def group_norm(n, m, v, centred):
                dve.wait_ge(gm_out, n)
                steps.did(dve.tensor_copy(g_mean[:, :], bank[6][:, 64:64 + NB]))
                steps.then(tt(centred, m, bank[6][:, 64:64 + NB], ALU.subtract))
                steps.then(tt(t4, centred, centred, ALU.mult))
                tt(t5, t4, v, ALU.add).then_inc(gm_in, 1)
                dve.wait_ge(std_ready, n)
                steps.then(dve.reciprocal(small[:, 7, :], small[:, 0, :]))

            group_norm(1, mean[:, :], var[:, :], t0)
            steps.then(tt(t1, t0, small[:, 7, :], ALU.mult))
            steps.did(tt(nan_mask[:, :], t1, t1, ALU.is_equal))
            steps.then(dve.memset(t2, 0.0))
            steps.then(dve.copy_predicated(t2, nan_mask[:, :], t1))
            dve.tensor_scalar(k_in[:, 0, :], t2, FMAX, -FMAX, ALU.min, ALU.max).then_inc(kan_in, 1)
            dve.wait_ge(kan_in, 1)

            def kan_layer(layer, n, grid):
                s = k_in[0:n, 0, :].unsqueeze(1)
                full = [n, KNOTS, NB]
                tt(k_dist[0:n, :, :], s.broadcast_to(full), grid.unsqueeze(2).broadcast_to(full), ALU.subtract).then_inc(dist_ready, 1)
                dve.wait_ge(dist_ready, layer + 1)
                steps.then(dve.tensor_scalar(k_ge[0:n, :, :], k_dist[0:n, :, :], 0.0, None, ALU.is_ge))
                steps.then(dve.scalar_tensor_tensor(out=k_bas[0:n, :, :], in0=k_dist[0:n, 1:KNOTS, :], scalar=0.0,
                                                    in1=k_ge[0:n, 0:KNOTS - 1, :], op0=ALU.is_lt, op1=ALU.mult))
                for k in range(1, ORDER + 1):
                    m = KNOTS - k
                    dve.wait_ge(rel_ready, ORDER * layer + k)
                    steps.then(tt(k_t[0:n, 0:m, :], k_rel[0:n, k - 1, 0:m, :], k_bas[0:n, 0:m, :], ALU.mult))
                    steps.then(tt(k_u[0:n, 0:m - 1, :], k_t[0:n, 0:m - 1, :], k_t[0:n, 1:m, :], ALU.subtract))
                    if k < ORDER:
                        steps.then(tt(k_bas[0:n, 0:m - 1, :], k_u[0:n, 0:m - 1, :], k_bas[0:n, 1:m, :], ALU.add))
                    else:
                        tt(k_rhs[0:n, 0:NK, :], k_u[0:n, 0:NK, :], k_bas[0:n, 1:m, :], ALU.add).then_inc(kan_rhs, 1)
                dve.wait_ge(kan_sig, 1 + 2 * layer)
                tt(k_rhs[0:n, NK, :], k_in[0:n, 0, :], k_in[0:n, 1, :], ALU.mult).then_inc(kan_rhs, 1)

            kan_layer(0, C, grid1_sb)
            dve.wait_ge(kan_sig, 2)
            tt(k_in[0:KH, 0, :], bank[7][0:KH, 0:NB], k_in[0:KH, 1, :], ALU.mult).then_inc(kan_in, 1)
            dve.wait_ge(kan_in, 2)
            kan_layer(1, KH, grid2_sb)
            dve.wait_ge(kan_sig, 4)

            ca, cb, cza, czb = (coef[:, n, :] for n in range(4))
            steps.then(tt(t1, k_in[:, 1, :], small[:, 7, :], ALU.mult))
            steps.did(dve.tensor_scalar(ca, t1, 1.0, None, ALU.add))
            steps.then(dve.scalar_tensor_tensor(out=cb, in0=g_mean[:, :], scalar=-1.0, in1=t1, op0=ALU.mult, op1=ALU.mult))
            steps.did(tt(t2, ca, mean[:, :], ALU.mult))
            steps.then(tt(t3, ca, ca, ALU.mult))
            steps.did(tt(var[:, :], t3, var[:, :], ALU.mult))
            tt(mean[:, :], t2, cb, ALU.add).then_inc(gm_in, 1)
            dve.wait_ge(gm_in, 3)
            steps.settle()
            group_norm(2, mean[:, :], var[:, :], t0)
            steps.did(tt(cza, ca, small[:, 7, :], ALU.mult))
            steps.then(tt(t1, cb, g_mean[:, :], ALU.subtract))
            steps.then(tt(czb, t1, small[:, 7, :], ALU.mult))
            dve.tensor_copy(eps[:, :], eps[:, :]).then_inc(coef_ready, 1)

            def z_low(it, u):
                base = it * IT
                for k in range(IT):
                    steps.did(dve.tensor_scalar(z32[:, k, :], one(x_all, base + k), one(cza.unsqueeze(2), base + k),
                                                one(czb.unsqueeze(2), base + k), ALU.mult, ALU.add))
                steps.settle()
                dve.wait_ge(zh_ready, base + IT)
                inner = zpad[u][:, :, :, 1:SIDE + 1, 1:SIDE + 1]
                z4 = z32[:, :, :].rearrange("p k (h w) -> p k h w", w=SIDE)
                tt(inner[:, 1], z4, inner[:, 0], ALU.subtract).then_inc(zl_ready, 1)
                for k in range(IT):
                    steps.did(dve.tensor_scalar(one(x_all, base + k), one(x_all, base + k), one(ca.unsqueeze(2), base + k),
                                                one(cb.unsqueeze(2), base + k), ALU.mult, ALU.add))
                steps.settle()
                dve.wait_ge(zl_ready, it + 1)
                kept = z_all[:, bass.ds(base, IT), :, :] if not isinstance(base, int) else z_all[:, base:base + IT, :, :]
                for part in range(2):
                    dve.tensor_copy(kept[:, :, part, :].rearrange("p k (h w) -> p k h w", w=SIDE),
                                    inner[:, part]).then_inc(z_kept, 1)

            def windows(it):
                dve.wait_ge(s1_ready, it + 1)
                flat = s1[:, :, :, :].rearrange("p j h w -> p (j h) w")
                mid = rows[:, 1, :, :].rearrange("p j h -> p (j h)")
                steps.then(dve.tensor_reduce(mid, flat, AX, ALU.add))
                steps.did(tt(rows[:, 0, :, :], rows[:, 1, :, :], s1[:, :, :, SIDE - 1], ALU.subtract))
                steps.then(tt(rows[:, 2, :, :], rows[:, 1, :, :], s1[:, :, :, 0], ALU.subtract))

                def at(ky):
                    w = win[:, ky]
                    return w[:, :, it, :] if isinstance(it, int) else w[:, :, bass.ds(it, 1), :].squeeze(2)
                steps.then(dve.tensor_reduce(at(1), rows[:, :, :, :], AX, ALU.add))
                steps.did(tt(at(0), at(1), rows[:, :, :, SIDE - 1], ALU.subtract))
                tt(at(2), at(1), rows[:, :, :, 0], ALU.subtract).then_inc(win_ready, 1)
                dve.wait_ge(win_ready, it + 1)
                steps.settle()
                dve.wait_ge(r2_ready, 2 * it + 2)
                dve.tensor_copy(one(r2_sum, it), r2_pair[:, :]).then_inc(r2_kept, 1)

            z_low(0, 0)
            z_low(1, 1)
            windows(0)
            start = steps.base + steps.n
            per = 2 * (2 * IT + 5)
            with dve.Fori(1, NIT // 2) as j:
                steps.enter(start - per, j, per)
                z_low(2 * j, 0)
                windows(2 * j - 1)
                z_low(2 * j + 1, 1)
                windows(2 * j)
            steps.leave(start, NIT // 2 - 1, per)
            windows(NIT - 1)

            dve.wait_ge(zeroed, 5)
            dve.wait_ge(r2_kept, NIT)
            win_b = win_p[:, :, :].rearrange("p q (n g j) -> p q n g j", g=2, j=2)
            taps = win[:, :, :, :, :].rearrange("p a b n j -> p (a b) n j")
            r2_b = r2_p[:, :].rearrange("p (n g j) -> p n g j", g=2, j=2)
            for g in range(2):
                rows_g = slice(HID * g, HID * g + HID)
                for u in range(2):
                    rows_u = slice(HID * u, HID * u + HID)
                    dve.tensor_scalar(win_b[rows_u, 0:4, :, g, :], taps[rows_g, u:8:2], 1.0 / HW, None, ALU.mult).then_inc(sums_ready, 1)
                dve.tensor_scalar(win_b[HID:P, 4, :, g, :], taps[rows_g, 8], 1.0 / HW, None, ALU.mult).then_inc(sums_ready, 1)
                dve.tensor_scalar(r2_b[:, :, g, :], r2_sum[rows_g, :, :], 1.0 / HW, None, ALU.mult).then_inc(sums_ready, 1)

            def halves(i):
                dve.wait_ge(sq_ready, i + 1)
                if not isinstance(i, int) or i >= 1:
                    dve.wait_ge(xt_done, i)
                dve.tensor_scalar(xp.rearrange("p t m -> p (t m)"), sq_v, star[:, 0:1],
                                  star[:, 1:2], ALU.mult, ALU.add).then_inc(xp_ready, 1)
                dve.wait_ge(xp_ready, i + 1)
                if not isinstance(i, int) or i >= 1:
                    dve.wait_ge(dft_done, i)
                    dve.wait_ge(eo_ready, i)
                steps.did(tt(eo[:, 0, :], xp[:, 0, :], xp[:, 1, :], ALU.add))
                steps.settle()
                tt(eo[:, 1, :], xp[:, 0, :], xp[:, 1, :], ALU.subtract).then_inc(eo_ready, 1)

            def terms(i):
                dve.wait_ge(spec_ready, i + 1)
                dve.wait_ge(w_done, i + 1)
                if not isinstance(i, int) or i >= 1:
                    dve.wait_ge(prod_ready, 2 * i)
                wide_shape = [P, 2, 2, P - 2]
                tt(t_re[:, :, :, 2:P], spec[:, :, :, 2:P], mixed_slot[:, :, 0, 2:P].unsqueeze(2).broadcast_to(wide_shape), ALU.mult).then_inc(terms_ready, 1)
                tt(t_im[:, :, :, 2:P], spec[:, :, :, 2:P], mixed_slot[:, :, 1, 2:P].unsqueeze(2).broadcast_to(wide_shape), ALU.mult).then_inc(terms_ready, 1)
                tt(t_re[:, :, :, 0:2], spec[:, :, :, 0:2], mixed_slot[:, :, :, 0:2], ALU.mult).then_inc(terms_ready, 1)

            def spatial(i):
                dve.wait_ge(sw_ready, i + 1)
                dve.wait_ge(xt_done, i + 1)
                if not isinstance(i, int) or i >= 1:
                    dve.wait_ge(sp_done, i)
                tt(qt[:, :, :], bank[2].rearrange("p (m s) -> p m s", m=2), swt[:, :, :], ALU.mult).then_inc(qt_ready, 1)

            def finish(i):
                dve.wait_ge(out_done, i + 1)
                tt(one(x_all, i), bank[6][:, 0:HW], one(x_all, i), ALU.add).then_inc(fin_ready, 1)

            halves(0)
            dve.wait_ge(logits_done, 1)
            steps.then(tt(logit, bank[7].rearrange("p (t b) -> p t b", b=NB),
                          bias_t.unsqueeze(2).broadcast_to([P, 16, NB]), ALU.add))
            by_filter = logit.rearrange("p (s f m) b -> p s f (m b)", s=2, f=NF)
            sm = rt_max[:, 0:2, :]
            over = [P, 2, NF, 2 * NB]
            steps.then(dve.tensor_reduce(sm, by_filter.rearrange("p s f q -> p s q f"), AX, ALU.max))
            tt(by_filter, by_filter, sm.unsqueeze(2).broadcast_to(over), ALU.subtract).then_inc(soft_in, 1)
            dve.wait_ge(soft_exp, 1)
            steps.then(dve.tensor_reduce(sm, by_filter.rearrange("p s f q -> p s q f"), AX, ALU.add))
            steps.then(dve.reciprocal(rt_max[:, 2:4, :], sm))
            steps.then(tt(by_filter, by_filter, rt_max[:, 2:4, :].unsqueeze(2).broadcast_to(over), ALU.mult))
            src = logit
            for part in range(3):
                g = LEFT_PART.index(part)
                own = rt_cols[:, :, :, g * 8:g * 8 + 8].rearrange("p b m c -> p c m b")
                src4 = src[:, :, :].rearrange("p (c m) b -> p c m b", m=2)
                if part < 2:
                    dve.tensor_copy(rt_part[part][:, :, :], src[:, :, :]).then_inc(rt_ready, 1)
                    dve.wait_ge(rt_ready, part + 1)
                    steps.did(dve.tensor_copy(own, rt_part[part][:, :, :].rearrange("p (c m) b -> p c m b", m=2)))
                    steps.then(tt(rt_res, src[:, :, :], rt_part[part][:, :, :], ALU.subtract))
                    src = rt_res
                else:
                    dve.tensor_copy(own, src4).then_inc(rt_ready, 1)
            for n in range(1, NIT, 2):
                dve.wait_ge(rt_done, n + 1)
                dve.tensor_copy(route[0:8 * GROUPS, n * IT:(n + 1) * IT, :, :].rearrange("p b m c -> p (b m c)"),
                                bank[6][0:8 * GROUPS].bitcast(BF16)).then_inc(rt_out[1], 1)
            terms(0)
            halves(1)
            spatial(0)

            def round_of(i):
                terms(i + 1)
                halves(i + 2)
                spatial(i + 1)
                finish(i)

            round_of(0)
            start = steps.base + steps.n
            with dve.Fori(1, NB - 2) as i:
                steps.enter(start - 1, i, 1)
                round_of(i)
            steps.leave(start, NB - 3, 1)
            terms(NB - 1)
            spatial(NB - 1)
            finish(NB - 2)
            finish(NB - 1)

        @block.tensor
        def _(pe):
            mm = pe.matmul

            def turn(dst, src, n):
                return pe.transpose(dst, src, ident[0:n, 0:n])

            pe.wait_ge(in_sym, 16)
            for part in range(2):
                for k in range(4):
                    u, c = divmod(k, 2)
                    last = mm(bank[5][:, part * NF:(part + 1) * NF], sym_sb[:, u, c, part * P:(part + 1) * P],
                              cw_sb[:, u, c:2 * NF:2], start=(k == 0), stop=(k == 3))
            last.then_inc(filt_done, 1)
            pe.wait_ge(in_early, 16)
            pe.wait_ge(max_cols, 3)
            turn(bank[6][0:3, 128:256], maxima[:, :], P).then_inc(max_rows, 1)
            pe.wait_ge(max_diag, 1)
            pe.wait_ge(const_set, 3)
            mm(bank[6][:, 256:259], ones[:, :], maxima_d[:, :], start=True, stop=True).then_inc(max_done, 1)
            pe.wait_ge(filt_cols, 2 * GROUPS)
            for n in range(4):
                last = pe.transpose(bank[4].bitcast(BF16)[:, n * P:(n + 1) * P], f_cols[:, n, :], ident_b[:, :])
            last.then_inc(filt_done, 1)

            def group_means(n):
                pe.wait_ge(gm_in, 2 * n - 1)
                mm(bank[6][:, 64:64 + NB], group, mean[:, :], start=True, stop=True).then_inc(gm_out, 1)
                pe.wait_ge(gm_in, 2 * n)
                mm(bank[6][:, 0:NB], group, small[:, 6, :], start=True, stop=True).then_inc(var_ready, 1)

            group_means(1)
            pe.wait_ge(kan_w_ready, 2)
            for layer, (n, w, dst) in enumerate(((C, kan1_t, bank[7][0:KH, 0:NB]), (KH, kan2_t, bank[7][:, 64:64 + NB]))):
                for k in range(NK + 1):
                    if k in (0, NK):
                        pe.wait_ge(kan_rhs, 2 * layer + 1 + k // NK)
                    last = mm(dst, w[:, k, :], k_rhs[0:n, k, :], start=(k == 0), stop=(k == NK))
                last.then_inc(kan_done, 1)
            group_means(2)

            pe.wait_ge(split_lo, 1)

            def branches(it, u):
                pe.wait_ge(zl_ready, it + 1)
                if not isinstance(it, int) or it >= 2:
                    pe.wait_ge(r1_ready, it - 1)
                    pe.wait_ge(s1_ready, it - 1)
                    pe.wait_ge(r2_ready, 2 * it - 2)
                passes = ((conv_h, 0), (conv_l, 0), (conv_h, 1))
                for n, (w, part) in enumerate(passes):
                    for g in range(2):
                        last = mm(bank[2 + u][HID * g:HID * g + HID, :], w[:, TAPS, :],
                                  zpad[u][:, part, 2 * g:2 * g + 2, 1:SIDE + 1, 1:SIDE + 1], start=(n == 0), stop=(n == 2))
                last.then_inc(rw1_done, 1)
                for n, (w, part) in enumerate(passes):
                    for t in range(TAPS):
                        dy, dx = divmod(t, 3)
                        for g in range(2):
                            last = mm(bank[u][HID * g:HID * g + HID, :], w[:, t, :],
                                      zpad[u][:, part, 2 * g:2 * g + 2, dy:dy + SIDE, dx:dx + SIDE],
                                      start=(n == 0 and t == 0), stop=(n == 2 and t == TAPS - 1))
                last.then_inc(conv_done, 1)
                pe.wait_ge(r1_ready, it + 1)
                mm(bank[5 + u], rwc_t, r1[:, :], start=True, stop=True).then_inc(rwc_done, 1)

            branches(0, 0)
            branches(1, 1)
            with pe.Fori(1, NIT // 2) as j:
                branches(2 * j, 0)
                branches(2 * j + 1, 1)

            def expand(i):
                if not isinstance(i, int) or i >= 1:
                    pe.wait_ge(relu_ready, i)
                z = one(z_all, i)
                for t in range(2):
                    cols = slice(t * P, (t + 1) * P)
                    for n, (part, w) in enumerate(((0, pw1_h), (1, pw1_h), (0, pw1_l))):
                        last = mm(bank[0][:, t * MED:(t + 1) * MED], z[:, part, cols], w, start=(n == 0), stop=(n == 2))
                last.then_inc(v_done, 1)

            def transform(i):
                pe.wait_ge(eo_ready, i + 1)
                if not isinstance(i, int) or i >= 1:
                    pe.wait_ge(spec_ready, i)
                dst = bank[1].rearrange("p (m a s) -> p m a s", m=2, a=2)
                for odd in range(2):
                    for m in range(2):
                        last = mm(dst[:, m, :, 64 * odd:64 * odd + 64], eo[:, odd, m * P:(m + 1) * P], forward[:, odd, :, :],
                                  start=True, stop=True)
                last.then_inc(dft_done, 1)
                if not isinstance(i, int) or i >= 1:
                    pe.wait_ge(qt_ready, i)
                for m in range(2):
                    for t in range(2):
                        last = turn(bank[2][:, m * HW + t * P:m * HW + (t + 1) * P], xp[:, t, m * P:(m + 1) * P], P)
                last.then_inc(xt_done, 1)

            def mix(i):
                if not isinstance(i, int) or i >= 1:
                    pe.wait_ge(terms_ready, 3 * i)
                    pe.wait_ge(sw_ready, i)
                r = one(route, i)
                for m in range(2):
                    for side in range(2):
                        last = mm(bank[3 + side][:, m * HW:(m + 1) * HW], r[:, m, :], filters[:, side * HW:(side + 1) * HW],
                                  start=True, stop=True)
                last.then_inc(w_done, 1)

            def reduce(i):
                pe.wait_ge(prod_ready, 2 * i + 2)
                if not isinstance(i, int) or i >= 1:
                    pe.wait_ge(y_ready, i)
                for part in range(2):
                    for m in range(2):
                        last = mm(bank[5][:, part * C:(part + 1) * C], prod[:, m, part, :], pw2_t[:, m, :],
                                  start=(m == 0), stop=(m == 1))
                last.then_inc(y_done, 1)

            def compose(i):
                pe.wait_ge(qt_ready, i + 1)
                if not isinstance(i, int) or i >= 1:
                    pe.wait_ge(fin_ready, i)
                for m in range(2):
                    last = mm(bank[6][:, 0:HW], pw2_t[:, m, :], qt[:, m, :], start=(m == 0), stop=False)
                last.then_inc(sp_done, 1)
                pe.wait_ge(y_ready, i + 1)
                for part in range(2):
                    last = mm(bank[6][:, 0:HW], y_sb[:, part, :], inverse[:, part, :], start=False, stop=(part == 1))
                last.then_inc(out_done, 1)

            pe.wait_ge(r2_ready, 2 * NIT)
            pe.wait_ge(z_kept, 2 * NIT)
            expand(0)
            pe.wait_ge(in_branch, 32)
            pe.wait_ge(sums_ready, 8)
            for t in range(8):
                mm(bank[7][:, 256 + t * NB:256 + (t + 1) * NB], rwf_t[:, t, :], r2_p[:, :], start=True, stop=True)
            for t in range(8):
                for p in range(PAIRS):
                    last = mm(bank[7][:, t * NB:(t + 1) * NB], sp_t[:, t, p, :], win_p[:, p, :], start=(p == 0), stop=(p == PAIRS - 1))
            last.then_inc(logits_done, 1)
            transform(0)
            expand(1)
            pe.wait_ge(rt_ready, 3)
            pe.wait_ge(rt_dup, 3)
            for n in range(NIT):
                if n >= 2:
                    pe.wait_ge(rt_out[n % 2], n // 2)
                for k in range(IT):
                    for m in range(2):
                        last = pe.transpose(bank[5 + n % 2].bitcast(BF16)[0:8 * GROUPS, (2 * k + m) * P:(2 * k + m + 1) * P],
                                            rt_cols[:, n * IT + k, m, :], ident_b[:, :])
                last.then_inc(rt_done, 1)
            pe.wait_ge(rt_out[0], NIT // 2)
            pe.wait_ge(rt_out[1], NIT // 2)
            pe.wait_ge(filt_ready, 1)
            mix(0)

            def round_of(i):
                expand(i + 2)
                transform(i + 1)
                mix(i + 1)
                reduce(i)
                compose(i)

            round_of(0)
            with pe.Fori(1, NB - 2) as i:
                round_of(i)
            transform(NB - 1)
            mix(NB - 1)
            reduce(NB - 2)
            compose(NB - 2)
            reduce(NB - 1)
            compose(NB - 1)


def packed(pack, rows, parts):
    assert list(parts) == list(pack)
    flat = [np.reshape(parts[name], (rows, pack[name])) for name in pack]
    return np.ascontiguousarray(np.concatenate(flat, axis=1))


def layout(inputs):
    given = {name.split("_conv_", 1)[-1]: np.asarray(a) for name, a in inputs.items()}
    con = {name: a.astype(np.float32) for name, a in constants().items()}
    twice = lambda a: np.concatenate([a, a])
    rwc = np.zeros((P, P), np.float32)
    rwc[:HID, :HID] = rwc[HID:, HID:] = given["rw_conv_w"][:, :, 0, 0].T
    early = packed(EARLY, P, {
        "ident": con["ident"], "group": con["group"], "grid1": given["grid1"],
        "spline1": given["spline_w1"].transpose(1, 2, 0), "base1": given["base_w1"].T, "scaler1": given["scaler1"].T,
    })
    kan2 = packed(KAN2, KH, {
        "grid2": given["grid2"], "spline2": given["spline_w2"].transpose(1, 2, 0),
        "base2": given["base_w2"].T, "scaler2": given["scaler2"].T,
    })
    later = packed(LATER, P, {
        "conv": given["sp_fc1_w"].reshape(HID, C, TAPS).transpose(1, 2, 0), "rw1": given["rw_fc1_w"][:, :, 0, 0].T,
        "pw1": given["w_pw1"].T, "rwc": rwc, "pw2": given["w_pw2"].reshape(C, 2, P).transpose(2, 1, 0),
        "logit_bias": np.concatenate([given["sp_fc2_b"], given["rw_fc2_b"]]).reshape(16, P).T,
        "hidden_bias": np.stack([twice(given[n]) for n in ("sp_fc1_b", "rw_fc1_b", "rw_conv_b")], axis=1),
        "star": np.broadcast_to(np.concatenate([given["star_scale"], given["star_bias"]]), (P, 2)),
        "forward": con["forward"], "inverse": con["inverse"],
        "pixel_filters": given["spatial_weights"].reshape(2, P, NF).transpose(1, 0, 2),
    })
    sym = packed(SYM, 72, {
        "sym": con["sym"], "filters": given["complex_weights"].reshape(2, 72, 2 * NF).transpose(1, 0, 2),
    })
    branch_r = given["rw_fc2_w"][:, :, 0, 0].T
    by_tap = given["sp_fc2_w"].reshape(8, P, HID, TAPS).transpose(3, 2, 0, 1)
    branch_s = np.stack([by_tap[pair_tap(p):pair_tap(p) + 2].reshape(2 * HID, 8, P) for p in range(PAIRS)], axis=2)
    return {"x": given["x"], "early": early, "kan2": kan2, "later": later, "sym": sym,
            "branch_r": np.ascontiguousarray(branch_r), "branch_s": branch_s.reshape(P, -1)}


def kernel(**inputs):
    import concourse.bacc as bacc
    from concourse.bass_utils import run_bass_kernel_spmd

    nc = bacc.Bacc("TRN2", target_bir_lowering=False, num_devices=1)
    arrays, args = {}, []
    for name, a in layout(inputs).items():
        arrays[f"in_{name}"] = a = np.ascontiguousarray(a)
        args.append(nc.dram_tensor(f"in_{name}", a.shape, mybir.dt.from_np(a.dtype), kind="ExternalInput").ap())
    args.append(nc.dram_tensor("out_0", (NB, C, SIDE, SIDE), F32, kind="ExternalOutput").ap())
    build(nc, *args)
    r = run_bass_kernel_spmd(nc, [arrays], core_ids=[0])
    return r.results[0]["out_0"]
```

```python
from contextlib import ExitStack

import numpy as np

import concourse.bass as bass
from concourse import mybir

F32 = mybir.dt.float32
F16 = mybir.dt.float16
BF16 = mybir.dt.bfloat16
I32 = mybir.dt.int32
ALU = mybir.AluOpType
ACT = mybir.ActivationFunctionType
AX = mybir.AxisListType.X

P = 128
NB = 32
C = 128
SIDE = 16
HW = SIDE * SIDE
MED = 2 * C
NF = 4
HID = 64
TAPS = 9
PAD = SIDE + 2
KH = 16
KNOTS = 12
ORDER = 3
NK = KNOTS - 1 - ORDER
GROUP = 4
EPS = 1e-5
FMAX = 3.4028235e38

IT = 4
NIT = NB // IT
PAIRS = 5
GROUPS = 6
LEFT_PART = [0, 0, 0, 1, 1, 2]
RIGHT_PART = [0, 1, 2, 0, 1, 0]
STACK = 16
X_CHUNKS = 8
HALF = NB // 2


def pair_tap(p):
    return min(2 * p, TAPS - 2)


def slots():
    inner = range(1, SIDE // 2)
    half = SIDE // 2
    found = [((0, 0), (0, half)), ((half, 0), (half, half))]
    for first in (0, 1):
        for ky in range(first, SIDE, 2):
            found += [((ky, kx), (ky, kx)) for kx in inner]
        for ky in range(first, half, 2):
            if ky:
                found += [((ky, kx), (ky, kx)) for kx in (0, half)]
    assert len(found) == P
    return found


def constants():
    half = SIDE // 2
    fs = half + 1
    ident = np.eye(P)
    group = np.kron(np.eye(P // GROUP), np.full((GROUP, GROUP), 1.0 / GROUP))
    h, w = np.divmod(np.arange(HW), SIDE)
    forward = np.zeros((P, 2, 2, 64))
    inverse = np.zeros((2, 64, 2, P))
    sym = np.zeros((SIDE, fs, 2, 2, P))
    for n, (fa, fb) in enumerate(slots()):
        odd, col = divmod(n, 64)
        real = fa != fb
        for part, (ky, kx) in enumerate((fa, fb)):
            angle = 2 * np.pi * (ky * h + kx * w) / SIDE
            wave = np.cos(angle) if real or part == 0 else -np.sin(angle)
            forward[:, odd, part, col] = wave[:P] / SIDE
            inverse[part, col, odd] = wave[:P] * (1 if real else 2) / SIDE
            re_im = 0 if real else part
            if real or kx not in (0, half):
                sym[ky, kx, re_im, part, n] = 1
            else:
                sym[ky, kx, re_im, part, n] = 0.5
                sym[(SIDE - ky) % SIDE, kx, re_im, part, n] = 0.5 if re_im == 0 else -0.5
    sym = sym.reshape(2, SIDE * fs // 2, 2, 2 * P).transpose(1, 0, 2, 3).reshape(SIDE * fs // 2, -1)
    return {
        "ident": ident, "group": group, "forward": forward.reshape(P, -1),
        "inverse": inverse.reshape(P, -1), "sym": sym,
    }


class Steps:

    def __init__(self, eng, sem):
        self.eng, self.sem, self.base, self.n = eng, sem, 0, 0

    def did(self, ins):
        ins.then_inc(self.sem, 1)
        self.n += 1

    def settle(self):
        self.eng.wait_ge(self.sem, self.base + self.n)

    def then(self, ins):
        self.did(ins)
        self.settle()

    def enter(self, start, i, per):
        self.base, self.n = start + i * per, 0

    def leave(self, start, rounds, per):
        assert self.n == per, self.n
        self.base, self.n = start + rounds * per, 0


EARLY = {"ident": P, "group": P, "grid1": KNOTS, "spline1": NK * KH, "base1": KH, "scaler1": KH}
KAN2 = {"grid2": KNOTS, "spline2": NK * C, "base2": C, "scaler2": C}
LATER = {"conv": TAPS * HID, "rw1": HID, "pw1": MED, "rwc": P, "pw2": MED, "logit_bias": 16, "hidden_bias": 3,
         "star": 2, "forward": 4 * 64, "inverse": 2 * P, "pixel_filters": 2 * NF}
SYM = {"sym": 4 * 2 * P, "filters": 2 * 2 * NF}


def columns(pack, name):
    lo = sum(list(pack.values())[:list(pack).index(name)])
    return slice(lo, lo + pack[name])


def build(nc, x, early, kan2, later, sym, branch_r, branch_s, out):
    ctx = ExitStack()
    with ctx:
        def sb(name, shape, dt=F32):
            return ctx.enter_context(nc.sbuf_tensor(name, shape, dt))

        def ps(name, shape, dt=F32):
            return ctx.enter_context(nc.psum_tensor(name, shape, dt))

        def sem(name):
            return ctx.enter_context(nc.semaphore(name))

        x_all = sb("x_all", [P, NB, HW])
        z_all = sb("z_all", [P, NB, 2, HW], F16)
        early_sb = sb("early_sb", [P, sum(EARLY.values())])
        kan2_sb = sb("kan2_sb", [KH, sum(KAN2.values())])
        later_sb = sb("later_sb", [P, sum(LATER.values())])
        sym_all = sb("sym_all", [72, sum(SYM.values())])

        def of(tensor, pack, name):
            return tensor[:, columns(pack, name)]

        ident, group = of(early_sb, EARLY, "ident"), of(early_sb, EARLY, "group")
        grid1_sb, grid2_sb = of(early_sb, EARLY, "grid1"), of(kan2_sb, KAN2, "grid2")
        kan1_t = early_sb[:, columns(EARLY, "spline1").start:columns(EARLY, "base1").stop].rearrange("c (k o) -> c k o", o=KH)
        kan2_t = kan2_sb[:, columns(KAN2, "spline2").start:columns(KAN2, "base2").stop].rearrange("c (k o) -> c k o", o=C)
        scaler1_sb, scaler2_sb = of(early_sb, EARLY, "scaler1"), of(kan2_sb, KAN2, "scaler2")
        rwc_t = of(later_sb, LATER, "rwc")
        pw2_t = of(later_sb, LATER, "pw2").rearrange("m (t d) -> m t d", t=2)
        bias_t, bias_col = of(later_sb, LATER, "logit_bias"), of(later_sb, LATER, "hidden_bias")
        star = of(later_sb, LATER, "star")
        forward = of(later_sb, LATER, "forward").rearrange("p (a b c) -> p a b c", a=2, b=2)
        inverse = of(later_sb, LATER, "inverse").rearrange("p (a s) -> p a s", a=2)
        sw_nat = of(later_sb, LATER, "pixel_filters").rearrange("p (u f) -> p u f", u=2)
        sym_sb = of(sym_all, SYM, "sym").rearrange("p (u c s) -> p u c s", u=2, c=2)
        cw_sb = of(sym_all, SYM, "filters").rearrange("p (u f) -> p u f", u=2)
        split_cols = TAPS * HID + HID + MED
        split_src = later_sb[:, 0:split_cols]
        spans = [columns(LATER, name) for name in ("conv", "rw1", "pw1")]
        split_h = sb("split_h", [P, split_cols], F16)
        split_l = sb("split_l", [P, split_cols], F16)
        conv_h, conv_l = (w[:, 0:(TAPS + 1) * HID].rearrange("p (t o) -> p t o", o=HID) for w in (split_h, split_l))
        pw1_h, pw1_l = (w[:, spans[2]] for w in (split_h, split_l))
        maxima = sb("maxima", [P, 3])
        maxima_t = sb("maxima_t", [3, P])
        maxima_d = sb("maxima_d", [3, 3])
        w_max = sb("w_max", [P, 3])
        w_inv = sb("w_inv", [P, 3])
        ones = sb("ones", [3, P])
        ident_b = sb("ident_b", [P, P], BF16)
        coef = sb("coef", [P, 4, NB])
        eps = sb("eps", [P, 1])
        scratch = sb("scratch", [P, 1])
        filters = sb("filters", [P, 512], BF16)
        rwf_t = sb("rwf_t", [HID, NF, MED])
        sp_t = sb("sp_t", [P, PAIRS, NF, MED])
        stats = sb("stats", [P, NB, 6])
        mean = sb("mean", [P, NB])
        var = sb("var", [P, NB])
        g_mean = sb("g_mean", [P, NB])
        small = sb("small", [P, 8, NB])
        nan_mask = sb("nan_mask", [P, NB], I32)
        k_inv = sb("k_inv", [P, 2, ORDER, KNOTS - 1])
        k_den = sb("k_den", [P, 2, ORDER, KNOTS - 1])
        k_in = sb("k_in", [P, 3, NB])
        k_dist = sb("k_dist", [P, KNOTS, NB])
        k_ge = sb("k_ge", [P, KNOTS, NB])
        k_rel = sb("k_rel", [P, ORDER, KNOTS - 1, NB])
        k_bas = sb("k_bas", [P, KNOTS - 1, NB])
        k_t = sb("k_t", [P, KNOTS - 1, NB])
        k_u = sb("k_u", [P, KNOTS - 1, NB])
        k_rhs = sb("k_rhs", [P, NK + 1, NB])
        zpads = sb("zpads", [P, 2, 2, IT, PAD, PAD], F16)
        zpad = [zpads[:, u] for u in range(2)]
        z32 = sb("z32", [P, IT, HW])
        r1 = sb("r1", [P, 512])
        s1 = sb("s1", [P, 2, SIDE, SIDE])
        r2 = sb("r2", [P, 2, HW], BF16)
        r2_pair = sb("r2_pair", [P, 2])
        r2_sum = sb("r2_sum", [P, NIT, 2])
        rows = sb("rows", [P, 3, 2, SIDE])
        win = sb("win", [P, 3, 3, NIT, 2])
        win_p = sb("win_p", [P, PAIRS, NB])
        r2_p = sb("r2_p", [HID, NB])
        rt_max = sb("rt_max", [P, 4, 2 * HALF])
        rt_part = [sb(f"rt_part{n}", [P, 16, HALF], BF16) for n in range(2)]
        f_cols = sb("f_cols", [P, 4, P], BF16)
        f_res = sb("f_res", [P, 4, NF])
        f_part = sb("f_part", [P, 3, 4, NF], BF16)
        by_image = sb("by_image", [P, 2, MED])
        logit = sb("logit", [P, 16, HALF])[:, :, :]
        rt_res = sb("rt_res", [P, 16, HALF])[:, :, :]
        rt_cols = sb("rt_cols", [P, NB, 2, P], BF16)
        relu_v, sq_v = (sb(name, [P, 512])[:, :] for name in ("relu_v", "sq_v"))
        route = sb("route", [P, 2, P], BF16)
        xp, eo, swt, qt = (sb(name, [P, 2, 256])[:, :, :] for name in ("xp", "eo", "swt", "qt"))
        spec, t_re, t_im = (sb(name, [P, 2, 2, P]) for name in ("spec", "t_re", "t_im"))
        prod = sb("prod", [P, 2, 2, 2, 64])
        y_sb = sb("y_sb", [P, 2, C])
        folded = sb("folded", [P, 2, P])
        waves = sb("waves", [P, 2, P])

        bank = [ps(f"bank{n}", [P, 512])[:, :] for n in range(8)]
        mixed_slot = bank[4].rearrange("p (m a s) -> p m a s", m=2, a=2)
        mixed_pixel = bank[3].rearrange("p (m s) -> p m s", m=2)

        in_x = [sem(f"in_x{n}") for n in range(X_CHUNKS)]
        in_early, in_kan2, in_later, in_sym, in_branch = (sem(n) for n in (
            "in_early", "in_kan2", "in_later", "in_sym", "in_branch"))
        zeroed, const_set, kan_w_ready, inv_ready = (sem(n) for n in ("zeroed", "const_set", "kan_w_ready", "inv_ready"))
        dve_step, pool_step = sem("dve_step"), sem("pool_step")
        max_cols, max_rows, max_diag, max_done, max_ready = (sem(n) for n in (
            "max_cols", "max_rows", "max_diag", "max_done", "max_ready"))
        scaled, split_hi, split_lo = sem("scaled"), sem("split_hi"), sem("split_lo")
        filt_done, filt_copied, filt_cols, filt_ready = (sem(n) for n in ("filt_done", "filt_copied", "filt_cols", "filt_ready"))
        dist_ready, rel_ready, gm_in, gm_out, var_ready, std_ready, kan_in, kan_sig, kan_rhs, kan_done, coef_ready = (
            [sem(f"{name}{half}") for half in range(2)] for name in (
                "dist_ready", "rel_ready", "gm_in", "gm_out", "var_ready", "std_ready", "kan_in", "kan_sig",
                "kan_rhs", "kan_done", "coef_ready"))
        tables_set = sem("tables_set")
        x1_ready, logits_read = sem("x1_ready"), sem("logits_read")
        zh_ready, zl_ready, z_kept = sem("zh_ready"), sem("zl_ready"), sem("z_kept")
        rw1_done, conv_done, rwc_done = sem("rw1_done"), sem("conv_done"), sem("rwc_done")
        r1_ready, s1_ready, r2_ready = sem("r1_ready"), sem("s1_ready"), sem("r2_ready")
        r2_kept, win_ready = sem("r2_kept"), sem("win_ready")
        sums_ready, logits_done, copied, turned, soft_in, soft_exp = (sem(n) for n in (
            "sums_ready", "logits_done", "copied", "turned", "soft_in", "soft_exp"))
        rt_ready, rt_dup, rt_done, rt_out = sem("rt_ready"), sem("rt_dup"), sem("rt_done"), sem("rt_out")
        v_done, relu_ready, sq_ready, xp_ready, eo_ready = (sem(n) for n in (
            "v_done", "relu_ready", "sq_ready", "xp_ready", "eo_ready"))
        dft_done, xt_done, w_done, spec_ready, sw_ready = (sem(n) for n in (
            "dft_done", "xt_done", "w_done", "spec_ready", "sw_ready"))
        terms_ready, prod_ready, qt_ready, y_done, y_ready = (sem(n) for n in (
            "terms_ready", "prod_ready", "qt_ready", "y_done", "y_ready"))
        sp_done, sp_added, folded_done, folded_ready, waves_ready, fin_ready, stored = (sem(n) for n in (
            "sp_done", "sp_added", "folded_done", "folded_ready", "waves_ready", "fin_ready", "stored"))

        def one(ap, n):
            if isinstance(n, int):
                return ap[:, n]
            return ap[:, bass.ds(n, 1)].squeeze(1)

        def half_of(half):
            return slice(half * HALF, (half + 1) * HALF)

        kan_bank = [bank[6], bank[7]]
        gm_var, gm_mean, kan_hid, kan_out = ([b[:, n * HALF:(n + 1) * HALF] for b in kan_bank] for n in (0, 2, 4, 6))

        block = ctx.enter_context(nc.Block())

        @block.sync
        def _(sp):
            k = NB // X_CHUNKS

            def load(n):
                sp.dma_start(x_all[:, n * k:(n + 1) * k, :],
                             x[n * k:(n + 1) * k].rearrange("b c h w -> c b (h w)")).then_inc(in_x[n], 16)

            sp.dma_start(early_sb[:, :], early).then_inc(in_early, 16)
            for n in range(X_CHUNKS // 2):
                load(n)
            sp.dma_start(later_sb[:, :], later).then_inc(in_later, 16)
            for n in range(X_CHUNKS // 2, X_CHUNKS):
                load(n)
            sp.dma_start(rwf_t[:, :, :], branch_r.rearrange("i (f m) -> i f m", f=NF)).then_inc(in_branch, 16)
            sp.dma_start(sp_t[:, :, :, :], branch_s.rearrange("i (q f m) -> i q f m", q=PAIRS, f=NF)).then_inc(in_branch, 16)
            out_v = out.rearrange("b c h w -> c b (h w)")
            with sp.Fori(0, NB) as i:
                sp.wait_ge(fin_ready, i + 1)
                sp.dma_start(one(out_v, i), one(x_all, i)).then_inc(stored, 16)
            sp.wait_ge(stored, 16 * NB)

        @block.gpsimd
        def _(pool):
            steps = Steps(pool, pool_step)
            pool.memset(f_cols[:, :, :], 0.0).then_inc(zeroed, 1)
            pool.memset(zpads[:, :, :, :, :, :], 0.0).then_inc(zeroed, 1)
            pool.memset(win_p[:, :, :], 0.0).then_inc(zeroed, 1)
            pool.memset(r2_p[:, :], 0.0).then_inc(zeroed, 1)
            pool.memset(t_im[:, :, :, :], 0.0).then_inc(zeroed, 1)
            pool.wait_ge(in_kan2, 16)
            pool.tensor_tensor(kan2_t[:, 0:NK, :], kan2_t[:, 0:NK, :],
                               scaler2_sb.unsqueeze(1).broadcast_to([KH, NK, C]), ALU.mult).then_inc(kan_w_ready, 1)
            pool.wait_ge(filt_copied, 1)
            pool.wait_ge(in_later, 16)
            steps.then(pool.tensor_copy(f_res[:, 2:4, :], sw_nat))
            for part in range(3):
                steps.then(pool.tensor_copy(f_part[:, part, :, :], f_res[:, :, :]))
                if part < 2:
                    steps.then(pool.tensor_tensor(f_res[:, :, :], f_res[:, :, :], f_part[:, part, :, :], ALU.subtract))
            pool.wait_ge(zeroed, 1)
            for g in range(GROUPS):
                for branch in range(2):
                    sides = slice(2 * branch, 2 * branch + 2)
                    start = 64 * (1 - branch) + g
                    pool.tensor_copy(f_cols[:, sides, start:64 * (2 - branch):STACK], f_part[:, RIGHT_PART[g], sides, :]).then_inc(filt_cols, 1)
            def places(half, layer):
                n = (C, KH)[layer]
                images = half_of(half)
                pool.wait_ge(inv_ready, 2)
                pool.wait_ge(dist_ready[half], layer + 1)
                for k in range(1, ORDER + 1):
                    m = KNOTS - k
                    pool.tensor_tensor(k_rel[0:n, k - 1, 0:m, images], k_dist[0:n, 0:m, images],
                                       k_inv[0:n, layer, k - 1, 0:m].unsqueeze(2).broadcast_to([n, m, HALF]), ALU.mult).then_inc(rel_ready[half], 1)

            places(0, 0)
            places(0, 1)
            pool.wait_ge(split_hi, 1)
            pool.tensor_tensor(split_l[:, :], split_src, split_h[:, :], ALU.subtract).then_inc(split_lo, 1)

            places(1, 0)

            def residual(it):
                pool.wait_ge(zl_ready, it + 1)
                images = slice(it * IT, it * IT + IT) if isinstance(it, int) else bass.ds(it * IT, IT)
                for n, op in enumerate((ALU.mult, ALU.add)):
                    pool.tensor_tensor(x_all[:, images, :], x_all[:, images, :],
                                       coef[:, n, images].unsqueeze(2).broadcast_to([P, IT, HW]), op).then_inc(x1_ready, 1)
                    if n == 0:
                        pool.wait_ge(x1_ready, 2 * it + 1)

            residual(0)
            places(1, 1)
            pool.memset(rt_cols[:, :, :, :], 0.0).then_inc(zeroed, 1)
            with pool.Fori(1, NIT) as it:
                residual(it)

            def products(i):
                pool.wait_ge(terms_ready, 3 * i + 3)
                if not isinstance(i, int) or i >= 1:
                    pool.wait_ge(y_done, i)
                halved = [t[:, :, :, :].rearrange("p m a (o s) -> p m a o s", o=2) for t in (t_re, t_im)]
                pool.tensor_tensor(prod[:, :, :, 0, :], halved[0][:, :, 0], halved[1][:, :, 1], ALU.subtract).then_inc(prod_ready, 1)
                pool.tensor_tensor(prod[:, :, :, 1, :], halved[0][:, :, 1], halved[1][:, :, 0], ALU.add).then_inc(prod_ready, 1)

            def unfold(i):
                pool.wait_ge(folded_ready, i + 1)
                if not isinstance(i, int) or i >= 1:
                    pool.wait_ge(fin_ready, i)
                pool.tensor_tensor(waves[:, 0, :], folded[:, 0, :], folded[:, 1, :], ALU.add).then_inc(waves_ready, 1)
                pool.tensor_tensor(waves[:, 1, :], folded[:, 0, :], folded[:, 1, :], ALU.subtract).then_inc(waves_ready, 1)
                pool.wait_ge(waves_ready, 2 * i + 2)
                pool.wait_ge(sp_added, i + 1)
                pool.tensor_tensor(one(x_all, i), one(x_all, i), waves[:, :, :].rearrange("p u s -> p (u s)"), ALU.add).then_inc(fin_ready, 1)

            products(0)
            products(1)
            unfold(0)
            with pool.Fori(1, NB // 2) as j:
                for i in (2 * j, 2 * j + 1):
                    products(i)
                    unfold(i - 1)

        @block.scalar
        def _(act):
            act.dma_start(kan2_sb[:, :], kan2).then_inc(in_kan2, 16)
            act.dma_start(sym_all[:, :], sym).then_inc(in_sym, 16)
            tables = Steps(act, tables_set)

            def ahead(function):
                tables.settle()
                tables.did(act.activation(scratch[:, :], eps[:, 0:1], function))

            act.wait_ge(const_set, 1)
            ahead(ACT.Sqrt)
            act.wait_ge(filt_done, 1)
            act.activation(f_res[:, 0:2, :], bank[5][:, 0:2 * NF].rearrange("p (a f) -> p a f", a=2), ACT.Identity).then_inc(filt_copied, 1)

            def deviation(half, n):
                act.wait_ge(const_set, 1)
                act.wait_ge(var_ready[half], n)
                act.activation(small[:, 0, half_of(half)], gm_var[half], ACT.Sqrt, bias=eps[:, 0:1]).then_inc(std_ready[half], 1)

            def sigmoid_sum(half, layer):
                n, sums = ((KH, kan_hid), (C, kan_out))[layer]
                act.wait_ge(kan_done[half], layer + 1)
                act.activation(k_in[0:n, 1, half_of(half)], sums[half][0:n, :], ACT.Sigmoid).then_inc(kan_sig[half], 1)

            def sigmoid_in(half, layer):
                n = (C, KH)[layer]
                act.wait_ge(kan_in[half], layer + 1)
                act.activation(k_in[0:n, 1, half_of(half)], k_in[0:n, 0, half_of(half)], ACT.Sigmoid).then_inc(kan_sig[half], 1)

            deviation(0, 1)
            sigmoid_in(0, 0)
            sigmoid_sum(0, 0)
            sigmoid_in(0, 1)
            act.wait_ge(max_ready, 1)
            for n, span in enumerate(spans):
                act.activation(later_sb[:, span], later_sb[:, span], ACT.Identity, scale=w_inv[:, n:n + 1]).then_inc(scaled, 1)
            act.wait_ge(scaled, 3)
            act.activation(split_h[:, :], split_src, ACT.Identity).then_inc(split_hi, 1)
            act.wait_ge(filt_done, 2)
            act.activation(filters[:, :], bank[4].bitcast(BF16)[:, 0:512], ACT.Identity).then_inc(filt_ready, 1)
            sigmoid_sum(0, 1)
            ahead(ACT.Sqrt)
            deviation(0, 2)

            def z_high(it, u):
                if not isinstance(it, int) or it >= 2:
                    act.wait_ge(conv_done, it - 1)
                    act.wait_ge(rw1_done, it - 1)
                    act.wait_ge(z_kept, 2 * it - 2)
                for k in range(IT):
                    b = it * IT + k
                    act.activation(zpad[u][:, 0, k, 1:SIDE + 1, 1:SIDE + 1],
                                   one(x_all, b).rearrange("p (h w) -> p h w", w=SIDE), ACT.Identity,
                                   bias=one(coef[:, 3, :].unsqueeze(2), b),
                                   scale=one(coef[:, 2, :].unsqueeze(2), b)).then_inc(zh_ready, 1)

            def hidden(it, u):
                act.wait_ge(rw1_done, it + 1)
                if not isinstance(it, int) or it >= 1:
                    act.wait_ge(rwc_done, it)
                act.activation(r1[:, :], bank[2 + u], ACT.Relu, bias=bias_col[:, 1:2], scale=w_max[:, 1:2]).then_inc(r1_ready, 1)
                act.wait_ge(conv_done, it + 1)
                if not isinstance(it, int) or it >= 1:
                    act.wait_ge(win_ready, it)
                    act.wait_ge(r2_kept, it)
                act.activation(s1[:, :, :, :].rearrange("p j h w -> p (j h w)"), bank[u], ACT.Relu,
                               bias=bias_col[:, 0:1], scale=w_max[:, 0:1]).then_inc(s1_ready, 1)

            def second_hidden(it, u):
                act.wait_ge(rwc_done, it + 1)
                if not isinstance(it, int) or it >= 1:
                    act.wait_ge(r2_ready, 2 * it)
                for j in range(2):
                    act.activation(r2[:, j, :], bank[5 + u][:, j * HW:(j + 1) * HW], ACT.Relu,
                                   bias=bias_col[:, 2:3], accum_out=r2_pair[:, j:j + 1]).then_inc(r2_ready, 1)

            act.wait_ge(zeroed, 2)
            act.wait_ge(coef_ready[0], 1)
            z_high(0, 0)
            deviation(1, 1)
            sigmoid_in(1, 0)
            z_high(1, 1)
            sigmoid_sum(1, 0)
            hidden(0, 0)
            second_hidden(0, 0)
            sigmoid_in(1, 1)
            z_high(2, 0)
            sigmoid_sum(1, 1)
            ahead(ACT.Sqrt)
            hidden(1, 1)
            second_hidden(1, 1)
            deviation(1, 2)
            ahead(ACT.Exp)
            act.wait_ge(coef_ready[1], 1)
            with act.Fori(1, 3) as j:
                z_high(2 * j + 1, 1)
                hidden(2 * j, 0)
                second_hidden(2 * j, 0)
                z_high(2 * j + 2, 0)
                hidden(2 * j + 1, 1)
                second_hidden(2 * j + 1, 1)

            def logits_copy(half):
                act.wait_ge(logits_done, half + 1)
                if half:
                    act.wait_ge(turned, 1)
                act.activation(by_image[:, :, :].rearrange("p s m -> p (s m)"), bank[7 - half], ACT.Identity).then_inc(copied, 1)

            def exponentials(half):
                act.wait_ge(soft_in, half + 1)
                act.activation(logit, logit, ACT.Exp).then_inc(soft_exp, 1)

            def repeated_parts(half):
                for g in range(GROUPS):
                    part = LEFT_PART[g]
                    if g != LEFT_PART.index(part):
                        act.wait_ge(rt_ready, 3 * half + part + 1)
                        act.activation(rt_cols[:, half_of(half), :, g:P:STACK].rearrange("p b m c -> p c m b"),
                                       rt_part[part][:, :, :].rearrange("p (c m) b -> p c m b", m=2), ACT.Identity).then_inc(rt_dup, 1)

            def relu_square(i):
                act.wait_ge(v_done, i + 1)
                if not isinstance(i, int) or i >= 1:
                    act.wait_ge(sq_ready, i)
                act.activation(relu_v[:, :], bank[0], ACT.Relu, scale=w_max[:, 2:3]).then_inc(relu_ready, 1)
                act.wait_ge(relu_ready, i + 1)
                if not isinstance(i, int) or i >= 1:
                    act.wait_ge(xp_ready, i)
                act.activation(sq_v[:, :], relu_v[:, :], ACT.Square).then_inc(sq_ready, 1)

            def spectrum(i):
                act.wait_ge(dft_done, i + 1)
                if not isinstance(i, int) or i >= 1:
                    act.wait_ge(terms_ready, 3 * i)
                act.activation(spec[:, :, :, :].rearrange("p m a s -> p (m a s)"), bank[2], ACT.Identity).then_inc(spec_ready, 1)

            def spatial_mix(i):
                act.wait_ge(w_done, i + 1)
                if not isinstance(i, int) or i >= 1:
                    act.wait_ge(qt_ready, i)
                act.activation(swt[:, :, :], mixed_pixel, ACT.Identity).then_inc(sw_ready, 1)

            def route_copy(i):
                act.wait_ge(rt_done, i + 1)
                if not isinstance(i, int) or i >= 1:
                    act.wait_ge(w_done, i)
                act.activation(route[:, :, :], bank[7][:, 0:2 * P].rearrange("p (m c) -> p m c", m=2), ACT.Identity).then_inc(rt_out, 1)

            def y_copy(i):
                act.wait_ge(y_done, i + 1)
                if not isinstance(i, int) or i >= 1:
                    act.wait_ge(folded_done, i)
                act.activation(y_sb[:, :, :].rearrange("p a d -> p (a d)"), bank[1][:, 0:2 * C], ACT.Identity).then_inc(y_ready, 1)

            def folded_copy(i):
                act.wait_ge(folded_done, i + 1)
                if not isinstance(i, int) or i >= 1:
                    act.wait_ge(waves_ready, 2 * i)
                act.activation(folded[:, :, :].rearrange("p u s -> p (u s)"), bank[7][:, 2 * P:], ACT.Identity).then_inc(folded_ready, 1)

            logits_copy(0)
            z_high(7, 1)
            exponentials(0)
            hidden(6, 0)
            second_hidden(6, 0)
            relu_square(0)
            repeated_parts(0)
            spectrum(0)
            route_copy(0)
            relu_square(1)
            hidden(7, 1)
            spatial_mix(0)
            second_hidden(7, 1)
            route_copy(1)
            spectrum(1)
            relu_square(2)
            spatial_mix(1)
            route_copy(2)
            y_copy(0)
            folded_copy(0)

            def round_of(i):
                relu_square(i + 2)
                spectrum(i + 1)
                spatial_mix(i + 1)
                route_copy(i + 2)
                y_copy(i)
                folded_copy(i)

            relu_square(3)
            logits_copy(1)
            spectrum(2)
            spatial_mix(2)
            route_copy(3)
            y_copy(1)
            exponentials(1)
            folded_copy(1)
            round_of(2)
            round_of(3)
            repeated_parts(1)
            with act.Fori(2, NB // 2 - 1) as j:
                round_of(2 * j)
                round_of(2 * j + 1)
            spectrum(NB - 1)
            spatial_mix(NB - 1)
            y_copy(NB - 2)
            folded_copy(NB - 2)
            y_copy(NB - 1)
            folded_copy(NB - 1)

        @block.vector
        def _(dve):
            steps = Steps(dve, dve_step)
            tt = dve.tensor_tensor

            dve.memset(eps[:, :], EPS).then_inc(const_set, 1)
            dve.memset(ones[:, :], 1.0).then_inc(const_set, 1)
            dve.wait_ge(in_early, 16)
            tt(kan1_t[:, 0:NK, :], kan1_t[:, 0:NK, :],
               scaler1_sb.unsqueeze(1).broadcast_to([C, NK, KH]), ALU.mult).then_inc(kan_w_ready, 1)
            dve.tensor_copy(ident_b[:, :], ident).then_inc(const_set, 1)

            def inverses(layer, n, grid):
                for k in range(1, ORDER + 1):
                    steps.did(tt(k_den[0:n, layer, k - 1, 0:KNOTS - k], grid[:, k:KNOTS], grid[:, 0:KNOTS - k], ALU.subtract))
                steps.settle()
                for k in range(1, ORDER + 1):
                    last = dve.reciprocal(k_inv[0:n, layer, k - 1, 0:KNOTS - k], k_den[0:n, layer, k - 1, 0:KNOTS - k])
                    if k < ORDER:
                        steps.did(last)
                last.then_inc(inv_ready, 1)

            inverses(0, C, grid1_sb)
            dve.wait_ge(in_kan2, 16)
            inverses(1, KH, grid2_sb)

            def statistics(n):
                dve.wait_ge(in_x[n], 16)
                for b in range(n * NB // X_CHUNKS, (n + 1) * NB // X_CHUNKS):
                    steps.did(dve.bn_stats(stats[:, b, :], x_all[:, b, :]))

            t0, t1, t2, t3, t4, t5 = (small[:, n, :] for n in range(1, 7))

            def channel_stats(half):
                images = half_of(half)
                m_e, m_o, v_e, v_o = (stats[:, images, n] for n in (1, 4, 2, 5))
                steps.settle()
                steps.did(tt(t0[:, images], m_e, m_o, ALU.add))
                steps.did(tt(t1[:, images], m_e, m_o, ALU.subtract))
                steps.did(tt(t2[:, images], v_e, v_o, ALU.add))
                steps.settle()
                dve.tensor_scalar(mean[:, images], t0[:, images], 0.5, None, ALU.mult).then_inc(gm_in[half], 1)
                steps.then(dve.scalar_tensor_tensor(out=t3[:, images], in0=t1[:, images], scalar=0.25, in1=t1[:, images],
                                                    op0=ALU.mult, op1=ALU.mult))
                steps.did(dve.scalar_tensor_tensor(out=var[:, images], in0=t2[:, images], scalar=1.0 / HW, in1=t3[:, images],
                                                   op0=ALU.mult, op1=ALU.add))
                dve.wait_ge(gm_in[half], 1)

            def group_spread(half, n):
                images = half_of(half)
                dve.wait_ge(gm_out[half], n)
                steps.did(dve.tensor_copy(g_mean[:, images], gm_mean[half]))
                steps.then(tt(t0[:, images], mean[:, images], gm_mean[half], ALU.subtract))
                steps.then(tt(t4[:, images], t0[:, images], t0[:, images], ALU.mult))
                tt(t5[:, images], t4[:, images], var[:, images], ALU.add).then_inc(gm_in[half], 1)

            def inverse_deviation(half, n):
                images = half_of(half)
                dve.wait_ge(std_ready[half], n)
                steps.then(dve.reciprocal(small[:, 7, images], small[:, 0, images]))

            def kan_input(half):
                images = half_of(half)
                inverse_deviation(half, 1)
                steps.then(tt(t1[:, images], t0[:, images], small[:, 7, images], ALU.mult))
                steps.did(tt(nan_mask[:, images], t1[:, images], t1[:, images], ALU.is_equal))
                steps.then(dve.memset(t2[:, images], 0.0))
                steps.then(dve.copy_predicated(t2[:, images], nan_mask[:, images], t1[:, images]))
                dve.tensor_scalar(k_in[:, 0, images], t2[:, images], FMAX, -FMAX, ALU.min, ALU.max).then_inc(kan_in[half], 1)
                dve.wait_ge(kan_in[half], 1)

            def kan_layer(half, layer):
                n, grid = ((C, grid1_sb), (KH, grid2_sb))[layer]
                images = half_of(half)
                s = k_in[0:n, 0, images].unsqueeze(1)
                full = [n, KNOTS, HALF]
                tt(k_dist[0:n, :, images], s.broadcast_to(full), grid.unsqueeze(2).broadcast_to(full), ALU.subtract).then_inc(dist_ready[half], 1)
                dve.wait_ge(dist_ready[half], layer + 1)
                steps.then(dve.tensor_scalar(k_ge[0:n, :, images], k_dist[0:n, :, images], 0.0, None, ALU.is_ge))
                steps.then(dve.scalar_tensor_tensor(out=k_bas[0:n, :, images], in0=k_dist[0:n, 1:KNOTS, images], scalar=0.0,
                                                    in1=k_ge[0:n, 0:KNOTS - 1, images], op0=ALU.is_lt, op1=ALU.mult))
                for k in range(1, ORDER + 1):
                    m = KNOTS - k
                    dve.wait_ge(rel_ready[half], ORDER * layer + k)
                    steps.did(tt(k_t[0:n, 0:m - 1, images], k_rel[0:n, k - 1, 0:m - 1, images], k_bas[0:n, 0:m - 1, images], ALU.mult))
                    steps.then(dve.scalar_tensor_tensor(out=k_u[0:n, 0:m - 1, images], in0=k_rel[0:n, k - 1, 1:m, images], scalar=1.0,
                                                        in1=k_bas[0:n, 1:m, images], op0=ALU.subtract, op1=ALU.mult))
                    if k < ORDER:
                        steps.then(tt(k_bas[0:n, 0:m - 1, images], k_t[0:n, 0:m - 1, images], k_u[0:n, 0:m - 1, images], ALU.subtract))
                    else:
                        tt(k_rhs[0:n, 0:NK, images], k_t[0:n, 0:NK, images], k_u[0:n, 0:NK, images], ALU.subtract).then_inc(kan_rhs[half], 1)
                dve.wait_ge(kan_sig[half], 1 + 2 * layer)
                tt(k_rhs[0:n, NK, images], k_in[0:n, 0, images], k_in[0:n, 1, images], ALU.mult).then_inc(kan_rhs[half], 1)

            def kan_hidden(half):
                images = half_of(half)
                dve.wait_ge(kan_sig[half], 2)
                tt(k_in[0:KH, 0, images], kan_hid[half][0:KH, :], k_in[0:KH, 1, images], ALU.mult).then_inc(kan_in[half], 1)
                dve.wait_ge(kan_in[half], 2)

            def image_coefficients(half):
                ca, cb = (coef[:, n, half_of(half)] for n in range(2))
                images = half_of(half)
                dve.wait_ge(kan_sig[half], 4)
                steps.then(tt(t1[:, images], k_in[:, 1, images], small[:, 7, images], ALU.mult))
                steps.did(dve.tensor_scalar(ca, t1[:, images], 1.0, None, ALU.add))
                steps.then(dve.scalar_tensor_tensor(out=cb, in0=g_mean[:, images], scalar=-1.0, in1=t1[:, images], op0=ALU.mult, op1=ALU.mult))
                steps.did(tt(t2[:, images], ca, mean[:, images], ALU.mult))
                steps.then(tt(t3[:, images], ca, ca, ALU.mult))
                steps.did(tt(var[:, images], t3[:, images], var[:, images], ALU.mult))
                tt(mean[:, images], t2[:, images], cb, ALU.add).then_inc(gm_in[half], 1)
                dve.wait_ge(gm_in[half], 3)
                steps.settle()

            def z_coefficients(half):
                images = half_of(half)
                ca, cb, cza, czb = (coef[:, n, images] for n in range(4))
                inverse_deviation(half, 2)
                steps.did(tt(cza, ca, small[:, 7, images], ALU.mult))
                steps.then(tt(t1[:, images], cb, g_mean[:, images], ALU.subtract))
                tt(czb, t1[:, images], small[:, 7, images], ALU.mult).then_inc(coef_ready[half], 1)
                dve.wait_ge(coef_ready[half], 1)

            for n in range(X_CHUNKS // 2):
                statistics(n)
            channel_stats(0)
            group_spread(0, 1)
            dve.wait_ge(in_later, 16)
            for n, span in enumerate(spans):
                dve.tensor_reduce(maxima[:, n:n + 1], later_sb[:, span], AX, ALU.max, apply_absolute_value=True).then_inc(max_cols, 1)
            kan_input(0)
            kan_layer(0, 0)
            dve.wait_ge(max_rows, 1)
            steps.then(dve.tensor_reduce(maxima_t[:, 0:1], bank[0][0:3, 128:256], AX, ALU.max))
            dve.tensor_scalar(maxima_d[:, :], ident[0:3, 0:3], maxima_t[:, 0:1], None, ALU.mult).then_inc(max_diag, 1)
            kan_hidden(0)
            dve.wait_ge(max_done, 1)
            steps.then(dve.tensor_scalar(w_max[:, :], bank[0][:, 256:259], 1e-30, None, ALU.max))
            dve.reciprocal(w_inv[:, :], w_max[:, :]).then_inc(max_ready, 1)
            kan_layer(0, 1)
            statistics(4)
            statistics(5)
            image_coefficients(0)
            statistics(6)
            group_spread(0, 2)
            statistics(7)
            channel_stats(1)
            z_coefficients(0)
            group_spread(1, 1)

            cza, czb = coef[:, 2, :], coef[:, 3, :]

            def z_low(it, u):
                base = it * IT
                for k in range(IT):
                    steps.did(dve.tensor_scalar(z32[:, k, :], one(x_all, base + k), one(cza.unsqueeze(2), base + k),
                                                one(czb.unsqueeze(2), base + k), ALU.mult, ALU.add))
                steps.settle()
                dve.wait_ge(zh_ready, base + IT)
                inner = zpad[u][:, :, :, 1:SIDE + 1, 1:SIDE + 1]
                z4 = z32[:, :, :].rearrange("p k (h w) -> p k h w", w=SIDE)
                tt(inner[:, 1], z4, inner[:, 0], ALU.subtract).then_inc(zl_ready, 1)
                dve.wait_ge(zl_ready, it + 1)
                kept = z_all[:, bass.ds(base, IT), :, :] if not isinstance(base, int) else z_all[:, base:base + IT, :, :]
                for part in range(2):
                    dve.tensor_copy(kept[:, :, part, :].rearrange("p k (h w) -> p k h w", w=SIDE),
                                    inner[:, part]).then_inc(z_kept, 1)

            def windows(it):
                dve.wait_ge(s1_ready, it + 1)
                flat = s1[:, :, :, :].rearrange("p j h w -> p (j h) w")
                mid = rows[:, 1, :, :].rearrange("p j h -> p (j h)")
                steps.then(dve.tensor_reduce(mid, flat, AX, ALU.add))
                steps.did(tt(rows[:, 0, :, :], rows[:, 1, :, :], s1[:, :, :, SIDE - 1], ALU.subtract))
                steps.then(tt(rows[:, 2, :, :], rows[:, 1, :, :], s1[:, :, :, 0], ALU.subtract))

                def at(ky):
                    w = win[:, ky]
                    return w[:, :, it, :] if isinstance(it, int) else w[:, :, bass.ds(it, 1), :].squeeze(2)
                steps.then(dve.tensor_reduce(at(1), rows[:, :, :, :], AX, ALU.add))
                steps.did(tt(at(0), at(1), rows[:, :, :, SIDE - 1], ALU.subtract))
                tt(at(2), at(1), rows[:, :, :, 0], ALU.subtract).then_inc(win_ready, 1)
                dve.wait_ge(win_ready, it + 1)
                steps.settle()
                dve.wait_ge(r2_ready, 2 * it + 2)
                dve.tensor_copy(one(r2_sum, it), r2_pair[:, :]).then_inc(r2_kept, 1)

            z_low(0, 0)
            kan_input(1)
            kan_layer(1, 0)
            z_low(1, 1)
            kan_hidden(1)
            kan_layer(1, 1)
            windows(0)
            image_coefficients(1)
            group_spread(1, 2)
            z_low(2, 0)
            z_coefficients(1)
            start = steps.base + steps.n
            per = 2 * (IT + 5)
            with dve.Fori(1, 3) as j:
                steps.enter(start - per, j, per)
                windows(2 * j - 1)
                z_low(2 * j + 1, 1)
                windows(2 * j)
                z_low(2 * j + 2, 0)
            steps.leave(start, 2, per)

            def image_sums(half):
                dve.wait_ge(zeroed, 4)
                if half:
                    dve.wait_ge(logits_done, 1)
                its = slice(half * NIT // 2, (half + 1) * NIT // 2)
                dve.wait_ge(r2_kept, its.stop)
                win_b = win_p[:, :, :].rearrange("p q (n g j) -> p q n g j", g=2, j=2)[:, :, its]
                taps = win[:, :, :, :, :].rearrange("p a b n j -> p (a b) n j")[:, :, its]
                r2_b = r2_p[:, :].rearrange("p (n g j) -> p n g j", g=2, j=2)[:, its]
                for g in range(2):
                    rows_g = slice(HID * g, HID * g + HID)
                    for u in range(2):
                        rows_u = slice(HID * u, HID * u + HID)
                        dve.tensor_scalar(win_b[rows_u, 0:4, :, g, :], taps[rows_g, u:8:2], 1.0 / HW, None, ALU.mult).then_inc(sums_ready, 1)
                    dve.tensor_scalar(win_b[HID:P, 4, :, g, :], taps[rows_g, 8], 1.0 / HW, None, ALU.mult).then_inc(sums_ready, 1)
                    dve.tensor_scalar(r2_b[:, :, g, :], r2_sum[rows_g, its, :], 1.0 / HW, None, ALU.mult).then_inc(sums_ready, 1)

            by_filter = logit.rearrange("p (s f m) b -> p s f (m b)", s=2, f=NF)
            over = [P, 2, NF, 2 * HALF]
            sm = rt_max[:, 0:2, :]

            def logits(half):
                dve.wait_ge(turned, half + 1)
                tt(logit, bank[7 - half][:, 0:16 * HALF].rearrange("p (t b) -> p t b", b=HALF),
                   bias_t.unsqueeze(2).broadcast_to([P, 16, HALF]), ALU.add).then_inc(logits_read, 1)
                dve.wait_ge(logits_read, half + 1)
                steps.then(dve.tensor_reduce(sm, by_filter.rearrange("p s f q -> p s q f"), AX, ALU.max))
                tt(by_filter, by_filter, sm.unsqueeze(2).broadcast_to(over), ALU.subtract).then_inc(soft_in, 1)

            def routing(half):
                dve.wait_ge(soft_exp, half + 1)
                steps.then(dve.tensor_reduce(sm, by_filter.rearrange("p s f q -> p s q f"), AX, ALU.add))
                steps.then(dve.reciprocal(rt_max[:, 2:4, :], sm))
                steps.then(tt(by_filter, by_filter, rt_max[:, 2:4, :].unsqueeze(2).broadcast_to(over), ALU.mult))

            def routing_parts(half):
                dve.wait_ge(zeroed, 6)
                if half:
                    dve.wait_ge(rt_dup, 3)
                src = logit
                for part in range(3):
                    g = LEFT_PART.index(part)
                    own = rt_cols[:, half_of(half), :, g:P:STACK].rearrange("p b m c -> p c m b")
                    if part < 2:
                        dve.tensor_copy(rt_part[part][:, :, :], src).then_inc(rt_ready, 1)
                        dve.wait_ge(rt_ready, 3 * half + part + 1)
                        steps.did(dve.tensor_copy(own, rt_part[part][:, :, :].rearrange("p (c m) b -> p c m b", m=2)))
                        steps.then(tt(rt_res, src, rt_part[part][:, :, :], ALU.subtract))
                        src = rt_res
                    else:
                        dve.tensor_copy(own, src.rearrange("p (c m) b -> p c m b", m=2)).then_inc(rt_ready, 1)

            def halves(i):
                dve.wait_ge(sq_ready, i + 1)
                if not isinstance(i, int) or i >= 1:
                    dve.wait_ge(xt_done, i)
                dve.tensor_scalar(xp.rearrange("p t m -> p (t m)"), sq_v, star[:, 0:1],
                                  star[:, 1:2], ALU.mult, ALU.add).then_inc(xp_ready, 1)
                dve.wait_ge(xp_ready, i + 1)
                if not isinstance(i, int) or i >= 1:
                    dve.wait_ge(dft_done, i)
                    dve.wait_ge(eo_ready, i)
                steps.did(tt(eo[:, 0, :], xp[:, 0, :], xp[:, 1, :], ALU.add))
                steps.settle()
                tt(eo[:, 1, :], xp[:, 0, :], xp[:, 1, :], ALU.subtract).then_inc(eo_ready, 1)

            def terms(i):
                dve.wait_ge(spec_ready, i + 1)
                dve.wait_ge(w_done, i + 1)
                if not isinstance(i, int) or i >= 1:
                    dve.wait_ge(prod_ready, 2 * i)
                wide_shape = [P, 2, 2, P - 2]
                tt(t_re[:, :, :, 2:P], spec[:, :, :, 2:P], mixed_slot[:, :, 0, 2:P].unsqueeze(2).broadcast_to(wide_shape), ALU.mult).then_inc(terms_ready, 1)
                tt(t_im[:, :, :, 2:P], spec[:, :, :, 2:P], mixed_slot[:, :, 1, 2:P].unsqueeze(2).broadcast_to(wide_shape), ALU.mult).then_inc(terms_ready, 1)
                tt(t_re[:, :, :, 0:2], spec[:, :, :, 0:2], mixed_slot[:, :, :, 0:2], ALU.mult).then_inc(terms_ready, 1)

            def spatial(i):
                dve.wait_ge(sw_ready, i + 1)
                dve.wait_ge(xt_done, i + 1)
                if not isinstance(i, int) or i >= 1:
                    dve.wait_ge(sp_done, i)
                tt(qt[:, :, :], bank[5].rearrange("p (m s) -> p m s", m=2), swt[:, :, :], ALU.mult).then_inc(qt_ready, 1)

            def finish(i):
                dve.wait_ge(sp_done, i + 1)
                tt(one(x_all, i), bank[6][:, 0:HW], one(x_all, i), ALU.add).then_inc(sp_added, 1)

            image_sums(0)
            windows(5)
            logits(0)
            z_low(7, 1)
            routing(0)
            routing_parts(0)
            windows(6)
            halves(0)
            halves(1)
            terms(0)
            spatial(0)
            windows(7)
            image_sums(1)
            terms(1)
            dve.wait_ge(x1_ready, 2 * NIT)
            halves(2)
            finish(0)
            spatial(1)

            def round_of(i):
                halves(i + 2)
                terms(i + 1)
                spatial(i + 1)
                finish(i)

            logits(1)
            round_of(1)
            routing(1)
            round_of(2)
            routing_parts(1)
            round_of(3)

            start = steps.base + steps.n
            with dve.Fori(2, NB // 2 - 1) as j:
                steps.enter(start - 4, j, 2)
                round_of(2 * j)
                round_of(2 * j + 1)
            steps.leave(start, NB // 2 - 3, 2)
            terms(NB - 1)
            spatial(NB - 1)
            finish(NB - 2)
            finish(NB - 1)
            dve.wait_ge(folded_ready, NB)
            dve.wait_ge(fin_ready, NB - 1)
            steps.did(tt(waves[:, 0, :], folded[:, 0, :], folded[:, 1, :], ALU.add))
            steps.then(tt(waves[:, 1, :], folded[:, 0, :], folded[:, 1, :], ALU.subtract))
            dve.wait_ge(sp_added, NB)
            tt(x_all[:, NB - 1, :], x_all[:, NB - 1, :], waves[:, :, :].rearrange("p u s -> p (u s)"), ALU.add).then_inc(fin_ready, 1)

        @block.tensor
        def _(pe):
            mm = pe.matmul

            def turn(dst, src, n):
                return pe.transpose(dst, src, ident[0:n, 0:n])

            pe.wait_ge(in_sym, 16)
            for part in range(2):
                for k in range(4):
                    u, c = divmod(k, 2)
                    last = mm(bank[5][:, part * NF:(part + 1) * NF], sym_sb[:, u, c, part * P:(part + 1) * P],
                              cw_sb[:, u, c:2 * NF:2], start=(k == 0), stop=(k == 3))
            last.then_inc(filt_done, 1)
            def group_means(half, n):
                pe.wait_ge(gm_in[half], 2 * n - 1)
                mm(gm_mean[half], group, mean[:, half_of(half)], start=True, stop=True).then_inc(gm_out[half], 1)

            def group_variances(half, n):
                pe.wait_ge(gm_in[half], 2 * n)
                mm(gm_var[half], group, small[:, 6, half_of(half)], start=True, stop=True).then_inc(var_ready[half], 1)

            def kan_sums(half, layer):
                n, w, dst, outputs = ((C, kan1_t, kan_hid[half], KH), (KH, kan2_t, kan_out[half], C))[layer]
                pe.wait_ge(kan_w_ready, 2)
                for k in range(NK + 1):
                    if k in (0, NK):
                        pe.wait_ge(kan_rhs[half], 2 * layer + 1 + k // NK)
                    for o in range(0, outputs, 32):
                        outs = slice(o, min(o + 32, outputs))
                        last = mm(dst[outs, :], w[:, k, outs], k_rhs[0:n, k, half_of(half)], start=(k == 0), stop=(k == NK))
                last.then_inc(kan_done[half], 1)

            pe.wait_ge(in_early, 16)
            group_means(0, 1)
            group_variances(0, 1)
            pe.wait_ge(max_cols, 3)
            turn(bank[0][0:3, 128:256], maxima[:, :], P).then_inc(max_rows, 1)
            kan_sums(0, 0)
            pe.wait_ge(max_diag, 1)
            pe.wait_ge(const_set, 3)
            mm(bank[0][:, 256:259], ones[:, :], maxima_d[:, :], start=True, stop=True).then_inc(max_done, 1)
            pe.wait_ge(filt_cols, 2 * GROUPS)
            for n in range(4):
                last = pe.transpose(bank[4].bitcast(BF16)[:, n * P:(n + 1) * P], f_cols[:, n, :], ident_b[:, :])
            last.then_inc(filt_done, 1)
            kan_sums(0, 1)
            group_means(0, 2)
            group_variances(0, 2)

            pe.wait_ge(split_lo, 1)

            passes = ((conv_h, 0), (conv_l, 0), (conv_h, 1))

            def taps(it, u, n):
                w, part = passes[n]
                if n == 0:
                    pe.wait_ge(zh_ready, IT * it + IT)
                    if not isinstance(it, int) or it >= 2:
                        pe.wait_ge(r1_ready, it - 1)
                        pe.wait_ge(s1_ready, it - 1)
                        pe.wait_ge(r2_ready, 2 * it - 2)
                if n == 2:
                    pe.wait_ge(zl_ready, it + 1)
                for g in range(2):
                    last = mm(bank[2 + u][HID * g:HID * g + HID, :], w[:, TAPS, :],
                              zpad[u][:, part, 2 * g:2 * g + 2, 1:SIDE + 1, 1:SIDE + 1], start=(n == 0), stop=(n == 2))
                if n == 2:
                    last.then_inc(rw1_done, 1)
                for t in range(TAPS):
                    dy, dx = divmod(t, 3)
                    for g in range(2):
                        last = mm(bank[u][HID * g:HID * g + HID, :], w[:, t, :],
                                  zpad[u][:, part, 2 * g:2 * g + 2, dy:dy + SIDE, dx:dx + SIDE],
                                  start=(n == 0 and t == 0), stop=(n == 2 and t == TAPS - 1))
                if n == 2:
                    last.then_inc(conv_done, 1)

            def second_pointwise(it, u):
                pe.wait_ge(r1_ready, it + 1)
                mm(bank[5 + u], rwc_t, r1[:, :], start=True, stop=True).then_inc(rwc_done, 1)

            def branches(it, u):
                for n in range(3):
                    taps(it, u, n)
                second_pointwise(it, u)

            group_means(1, 1)
            group_variances(1, 1)
            for n in range(3):
                taps(0, 0, n)
            kan_sums(1, 0)
            taps(1, 1, 0)
            second_pointwise(0, 0)
            taps(1, 1, 1)
            kan_sums(1, 1)
            taps(1, 1, 2)
            group_means(1, 2)
            second_pointwise(1, 1)
            group_variances(1, 2)
            with pe.Fori(1, 3) as j:
                branches(2 * j, 0)
                branches(2 * j + 1, 1)

            def logits(half):
                pe.wait_ge(in_branch, 32)
                pe.wait_ge(sums_ready, 8 * (half + 1))
                for p in range(PAIRS):
                    for f in range(NF):
                        mm(bank[7 - half][NB * f:NB * f + NB, 0:MED], win_p[:, p, :], sp_t[:, p, f, :],
                           start=(p == 0), stop=(p == PAIRS - 1))
                for f in range(NF):
                    last = mm(bank[7 - half][NB * f:NB * f + NB, MED:2 * MED], r2_p[:, :], rwf_t[:, f, :], start=True, stop=True)
                last.then_inc(logits_done, 1)

            def turn_logits(half):
                pe.wait_ge(copied, half + 1)
                dst = bank[7 - half][:, 0:16 * HALF].rearrange("p (s f m b) -> p s m f b", s=2, f=NF, m=2)
                pick = ident.rearrange("p (f b) -> p f b", f=NF)[:, :, half * HALF:(half + 1) * HALF]
                for s in range(2):
                    for m in range(2):
                        last = mm(dst[:, s, m], by_image[:, s, m * P:(m + 1) * P], pick, start=True, stop=True)
                last.then_inc(turned, 1)

            logits(0)
            taps(6, 0, 0)
            def expand(i):
                if not isinstance(i, int) or i >= 1:
                    pe.wait_ge(relu_ready, i)
                z = one(z_all, i)
                for t in range(2):
                    cols = slice(t * P, (t + 1) * P)
                    for n, (part, w) in enumerate(((0, pw1_h), (1, pw1_h), (0, pw1_l))):
                        last = mm(bank[0][:, t * MED:(t + 1) * MED], z[:, part, cols], w, start=(n == 0), stop=(n == 2))
                last.then_inc(v_done, 1)

            def transform(i):
                pe.wait_ge(eo_ready, i + 1)
                if not isinstance(i, int) or i >= 1:
                    pe.wait_ge(spec_ready, i)
                dst = bank[2].rearrange("p (m a s) -> p m a s", m=2, a=2)
                for odd in range(2):
                    for m in range(2):
                        last = mm(dst[:, m, :, 64 * odd:64 * odd + 64], eo[:, odd, m * P:(m + 1) * P], forward[:, odd, :, :],
                                  start=True, stop=True)
                last.then_inc(dft_done, 1)
                if not isinstance(i, int) or i >= 1:
                    pe.wait_ge(qt_ready, i)
                for m in range(2):
                    for t in range(2):
                        last = turn(bank[5][:, m * HW + t * P:m * HW + (t + 1) * P], xp[:, t, m * P:(m + 1) * P], P)
                last.then_inc(xt_done, 1)

            def mix(i):
                pe.wait_ge(rt_out, i + 1)
                if not isinstance(i, int) or i >= 1:
                    pe.wait_ge(terms_ready, 3 * i)
                    pe.wait_ge(sw_ready, i)
                for m in range(2):
                    for side, rows in enumerate((slice(64, P), slice(0, 64))):
                        last = mm(bank[4 - side][:, m * HW:(m + 1) * HW], route[rows, m, :],
                                  filters[rows, side * HW:(side + 1) * HW], start=True, stop=True)
                last.then_inc(w_done, 1)

            def turn_route(i):
                if isinstance(i, int) and i == 0:
                    pe.wait_ge(rt_ready, 3)
                    pe.wait_ge(rt_dup, 3)
                if not isinstance(i, int) or i >= 1:
                    pe.wait_ge(rt_out, i)
                if not isinstance(i, int) or i >= 3:
                    pe.wait_ge(folded_ready, i - 2)
                cols = one(rt_cols, i)
                for m in range(2):
                    last = mm(bank[7][:, m * P:(m + 1) * P], cols[:, m, :], ident_b[:, :], start=True, stop=True)
                last.then_inc(rt_done, 1)

            def reduce(i):
                pe.wait_ge(prod_ready, 2 * i + 2)
                if not isinstance(i, int) or i >= 1:
                    pe.wait_ge(y_ready, i)
                for odd in range(2):
                    for m in range(2):
                        last = mm(bank[1][:, odd * C:(odd + 1) * C], prod[:, m, odd].rearrange("p a s -> p (a s)"), pw2_t[:, m, :],
                                  start=(m == 0), stop=(m == 1))
                last.then_inc(y_done, 1)

            def compose(i, turned_routes):
                pe.wait_ge(qt_ready, i + 1)
                if not isinstance(i, int) or i >= 1:
                    pe.wait_ge(sp_added, i)
                for m in range(2):
                    last = mm(bank[6][:, 0:HW], pw2_t[:, m, :], qt[:, m, :], start=(m == 0), stop=(m == 1))
                last.then_inc(sp_done, 1)
                pe.wait_ge(y_ready, i + 1)
                pe.wait_ge(rt_out, turned_routes)
                if not isinstance(i, int) or i >= 1:
                    pe.wait_ge(folded_ready, i)
                for odd in range(2):
                    last = mm(bank[7][:, (2 + odd) * P:(3 + odd) * P], y_sb[:, odd, :], inverse[:, odd, :], start=True, stop=True)
                last.then_inc(folded_done, 1)

            turn_logits(0)
            taps(6, 0, 1)
            taps(6, 0, 2)
            second_pointwise(6, 0)
            pe.wait_ge(z_kept, 2)
            pe.wait_ge(s1_ready, NIT - 1)
            expand(0)
            taps(NIT - 1, 1, 0)
            taps(NIT - 1, 1, 1)
            pe.wait_ge(r2_ready, 2 * NIT - 2)
            transform(0)
            pe.wait_ge(logits_read, 1)
            turn_route(0)
            expand(1)
            taps(NIT - 1, 1, 2)
            pe.wait_ge(filt_ready, 1)
            pe.wait_ge(r1_ready, NIT)
            mix(0)
            second_pointwise(NIT - 1, 1)
            turn_route(1)
            transform(1)
            expand(2)
            mix(1)
            turn_route(2)
            pe.wait_ge(s1_ready, NIT)
            reduce(0)
            pe.wait_ge(r2_ready, 2 * NIT)
            compose(0, 3)

            def round_of(i):
                expand(i + 2)
                transform(i + 1)
                mix(i + 1)
                turn_route(i + 2)
                reduce(i)
                compose(i, i + 3)

            expand(3)
            pe.wait_ge(sp_added, 1)
            logits(1)
            transform(2)
            turn_logits(1)
            mix(2)
            turn_route(3)
            reduce(1)
            pe.wait_ge(logits_read, 2)
            compose(1, 4)

            round_of(2)
            round_of(3)
            with pe.Fori(1, 3) as j:
                for n in range(4):
                    round_of(4 * j + n)
            pe.wait_ge(rt_ready, 6)
            pe.wait_ge(rt_dup, 6)
            with pe.Fori(3, NB // 4 - 1) as j:
                for n in range(4):
                    round_of(4 * j + n)
            round_of(NB - 4)
            round_of(NB - 3)
            transform(NB - 1)
            mix(NB - 1)
            reduce(NB - 2)
            compose(NB - 2, NB)
            reduce(NB - 1)
            compose(NB - 1, NB)


def packed(pack, rows, parts):
    assert list(parts) == list(pack)
    flat = [np.reshape(parts[name], (rows, pack[name])) for name in pack]
    return np.ascontiguousarray(np.concatenate(flat, axis=1))


def layout(inputs):
    given = {name.split("_conv_", 1)[-1]: np.asarray(a) for name, a in inputs.items()}
    con = {name: a.astype(np.float32) for name, a in constants().items()}
    twice = lambda a: np.concatenate([a, a])
    rwc = np.zeros((P, P), np.float32)
    rwc[:HID, :HID] = rwc[HID:, HID:] = given["rw_conv_w"][:, :, 0, 0].T
    early = packed(EARLY, P, {
        "ident": con["ident"], "group": con["group"], "grid1": given["grid1"],
        "spline1": given["spline_w1"].transpose(1, 2, 0), "base1": given["base_w1"].T, "scaler1": given["scaler1"].T,
    })
    kan2 = packed(KAN2, KH, {
        "grid2": given["grid2"], "spline2": given["spline_w2"].transpose(1, 2, 0),
        "base2": given["base_w2"].T, "scaler2": given["scaler2"].T,
    })
    later = packed(LATER, P, {
        "conv": given["sp_fc1_w"].reshape(HID, C, TAPS).transpose(1, 2, 0), "rw1": given["rw_fc1_w"][:, :, 0, 0].T,
        "pw1": given["w_pw1"].T, "rwc": rwc, "pw2": given["w_pw2"].reshape(C, 2, P).transpose(2, 1, 0),
        "logit_bias": np.concatenate([given["sp_fc2_b"], given["rw_fc2_b"]]).reshape(16, P).T,
        "hidden_bias": np.stack([twice(given[n]) for n in ("sp_fc1_b", "rw_fc1_b", "rw_conv_b")], axis=1),
        "star": np.broadcast_to(np.concatenate([given["star_scale"], given["star_bias"]]), (P, 2)),
        "forward": con["forward"], "inverse": con["inverse"],
        "pixel_filters": given["spatial_weights"].reshape(2, P, NF).transpose(1, 0, 2),
    })
    sym = packed(SYM, 72, {
        "sym": con["sym"], "filters": given["complex_weights"].reshape(2, 72, 2 * NF).transpose(1, 0, 2),
    })
    branch_r = given["rw_fc2_w"][:, :, 0, 0].T
    by_tap = given["sp_fc2_w"].reshape(NF * MED, HID, TAPS).transpose(2, 1, 0)
    branch_s = np.stack([by_tap[pair_tap(p):pair_tap(p) + 2].reshape(2 * HID, NF * MED) for p in range(PAIRS)], axis=1)
    return {"x": given["x"], "early": early, "kan2": kan2, "later": later, "sym": sym,
            "branch_r": np.ascontiguousarray(branch_r), "branch_s": branch_s.reshape(P, -1)}


def kernel(**inputs):
    import concourse.bacc as bacc
    from concourse.bass_utils import run_bass_kernel_spmd

    nc = bacc.Bacc("TRN2", target_bir_lowering=False, num_devices=1)
    arrays, args = {}, []
    for name, a in layout(inputs).items():
        arrays[f"in_{name}"] = a = np.ascontiguousarray(a)
        args.append(nc.dram_tensor(f"in_{name}", a.shape, mybir.dt.from_np(a.dtype), kind="ExternalInput").ap())
    args.append(nc.dram_tensor("out_0", (NB, C, SIDE, SIDE), F32, kind="ExternalOutput").ap())
    build(nc, *args)
    r = run_bass_kernel_spmd(nc, [arrays], core_ids=[0])
    return r.results[0]["out_0"]
```
